# Optimizing a Trainium2 kernel written in Bass

```python
import numpy as np
import jax
import jax.numpy as jnp

def _softmax(x, axis=-1):
    return jax.nn.softmax(x, axis=axis)

def _gelu(x):
    return jax.nn.gelu(x, approximate=True)

def _silu(x):
    return jax.nn.silu(x)

def _sigmoid(x):
    return jax.nn.sigmoid(x)

def _layernorm(x, axis=-1, eps=1e-05):
    m = jnp.mean(x, axis=axis, keepdims=True)
    v = jnp.var(x, axis=axis, keepdims=True)
    return (x - m) / jnp.sqrt(v + eps)

def _scatter_add(tgt, idx, src, axis=0):
    return tgt.at[idx].add(src)

def _segment_sum(src, seg, n):
    return jax.ops.segment_sum(src, seg, n)
kernel_name = 'mk_conv_attn_hybrid_d2_conv_nchw256_r4_00a84d'

def setup_inputs(seed: int=0):
    np.random.seed(seed)
    _w = jnp.asarray

    def _rec_inputs():
        import jax
        import jax.numpy as jnp
        _gk = jax.random.key(seed)
        x = -0.0002928 + 1 * jax.random.normal(jax.random.fold_in(_gk, 1), (4, 64, 16, 16), jnp.float32)
        return x
    x = _rec_inputs()

    def _L0_conv_setup():
        import jax, jax.numpy as jnp
        import numpy as np
        B, C, CI, H, W = (4, 64, 32, 16, 16)

        def conv1x1(x, w, b):
            return jnp.einsum('bchw,oc->bohw', x, w) + b[None, :, None, None]
        key = jax.random.key(seed)
        ks = jax.random.split(key, 9)
        s = 0.02
        return {'x': jax.random.normal(ks[0], (B, C, H, W), dtype=jnp.float32), 'Wg': jax.random.normal(ks[1], (CI, C), dtype=jnp.float32) * s, 'bg': jnp.zeros((CI,), dtype=jnp.float32), 'Wt': jax.random.normal(ks[2], (CI, C), dtype=jnp.float32) * s, 'bt': jnp.zeros((CI,), dtype=jnp.float32), 'Wp': jax.random.normal(ks[3], (CI, C), dtype=jnp.float32) * s, 'bp': jnp.zeros((CI,), dtype=jnp.float32), 'Wo': jax.random.normal(ks[4], (C, CI), dtype=jnp.float32) * s, 'bo': jnp.zeros((C,), dtype=jnp.float32)}
    _L0_conv_all = _L0_conv_setup()
    _L0_conv_in = {k: v for k, v in _L0_conv_all.items() if k in ('Wg', 'bg', 'Wt', 'bt', 'Wp', 'bp', 'Wo', 'bo')}
    del _L0_conv_all

    def _L1_attn_setup():
        import jax, jax.numpy as jnp
        import numpy as np
        N_HEAD = 4
        key = jax.random.key(seed)
        k1, k2, k3 = jax.random.split(key, 3)
        B, T, C = (8, 512, 64)
        x = jax.random.normal(k1, (B, T, C), dtype=jnp.float32)
        W_attn = jax.random.normal(k2, (C, 3 * C), dtype=jnp.float32) / np.sqrt(C)
        W_proj = jax.random.normal(k3, (C, C), dtype=jnp.float32) / np.sqrt(C)
        return {'x': x, 'W_attn': W_attn, 'W_proj': W_proj}
    _L1_attn_all = _L1_attn_setup()
    _L1_attn_in = {k: v for k, v in _L1_attn_all.items() if k in ('W_attn', 'W_proj')}
    del _L1_attn_all

    def _L1_ffn_setup():
        import jax, jax.numpy as jnp
        import numpy as np
        BN_EPS = 0.001

        def _bn(h, g, b, m, v):
            return g * (h - m) * jax.lax.rsqrt(v + BN_EPS) + b
        key = jax.random.key(seed)
        ks = jax.random.split(key, 8)
        B, F, Df = (64, 16, 64)
        E, H, D = (8, 64, 64)
        s1 = 1.0 / np.sqrt(Df)
        s2 = 1.0 / np.sqrt(H)
        return {'x': jax.random.normal(ks[0], (B, F, Df), jnp.float32), 'Wr': jax.random.normal(ks[1], (Df, E), jnp.float32) * s1, 'br': jnp.zeros((E,), jnp.float32), 'W1': jax.random.normal(ks[2], (E, Df, H), jnp.float32) * s1, 'b1': jnp.zeros((E, H), jnp.float32), 'g1': jnp.ones((E, H), jnp.float32), 'be1': jnp.zeros((E, H), jnp.float32), 'm1': jnp.zeros((E, H), jnp.float32), 'v1': jnp.ones((E, H), jnp.float32), 'W2': jax.random.normal(ks[3], (E, H, H), jnp.float32) * s2, 'b2': jnp.zeros((E, H), jnp.float32), 'g2': jnp.ones((E, H), jnp.float32), 'be2': jnp.zeros((E, H), jnp.float32), 'm2': jnp.zeros((E, H), jnp.float32), 'v2': jnp.ones((E, H), jnp.float32), 'Wo': jax.random.normal(ks[4], (E, H, D), jnp.float32) * s2, 'bo': jnp.zeros((E, D), jnp.float32)}
    _L1_ffn_all = _L1_ffn_setup()
    _L1_ffn_in = {k: v for k, v in _L1_ffn_all.items() if k in ('Wr', 'br', 'W1', 'b1', 'g1', 'be1', 'm1', 'v1', 'W2', 'b2', 'g2', 'be2', 'm2', 'v2', 'Wo', 'bo')}
    del _L1_ffn_all
    return {'x': x, 'L0_conv_Wg': _L0_conv_in['Wg'], 'L0_conv_bg': _L0_conv_in['bg'], 'L0_conv_Wt': _L0_conv_in['Wt'], 'L0_conv_bt': _L0_conv_in['bt'], 'L0_conv_Wp': _L0_conv_in['Wp'], 'L0_conv_bp': _L0_conv_in['bp'], 'L0_conv_Wo': _L0_conv_in['Wo'], 'L0_conv_bo': _L0_conv_in['bo'], 'L1_attn_W_attn': _L1_attn_in['W_attn'], 'L1_attn_W_proj': _L1_attn_in['W_proj'], 'L1_ffn_Wr': _L1_ffn_in['Wr'], 'L1_ffn_br': _L1_ffn_in['br'], 'L1_ffn_W1': _L1_ffn_in['W1'], 'L1_ffn_b1': _L1_ffn_in['b1'], 'L1_ffn_g1': _L1_ffn_in['g1'], 'L1_ffn_be1': _L1_ffn_in['be1'], 'L1_ffn_m1': _L1_ffn_in['m1'], 'L1_ffn_v1': _L1_ffn_in['v1'], 'L1_ffn_W2': _L1_ffn_in['W2'], 'L1_ffn_b2': _L1_ffn_in['b2'], 'L1_ffn_g2': _L1_ffn_in['g2'], 'L1_ffn_be2': _L1_ffn_in['be2'], 'L1_ffn_m2': _L1_ffn_in['m2'], 'L1_ffn_v2': _L1_ffn_in['v2'], 'L1_ffn_Wo': _L1_ffn_in['Wo'], 'L1_ffn_bo': _L1_ffn_in['bo']}

def reference(x, L0_conv_Wg, L0_conv_bg, L0_conv_Wt, L0_conv_bt, L0_conv_Wp, L0_conv_bp, L0_conv_Wo, L0_conv_bo, L1_attn_W_attn, L1_attn_W_proj, L1_ffn_Wr, L1_ffn_br, L1_ffn_W1, L1_ffn_b1, L1_ffn_g1, L1_ffn_be1, L1_ffn_m1, L1_ffn_v1, L1_ffn_W2, L1_ffn_b2, L1_ffn_g2, L1_ffn_be2, L1_ffn_m2, L1_ffn_v2, L1_ffn_Wo, L1_ffn_bo):
    import jax
    import jax.numpy as jnp

    def _L0_conv_ref(x, Wg, bg, Wt, bt, Wp, bp, Wo, bo):
        import jax, jax.numpy as jnp
        import numpy as np
        B, C, CI, H, W = (4, 64, 32, 16, 16)

        def conv1x1(x, w, b):
            return jnp.einsum('bchw,oc->bohw', x, w) + b[None, :, None, None]
        b, c, h, w = x.shape
        n = h * w
        g = conv1x1(x, Wg, bg).reshape(b, -1, n)
        th = conv1x1(x, Wt, bt).reshape(b, -1, n)
        ph = conv1x1(x, Wp, bp).reshape(b, -1, n)
        f = jnp.einsum('bci,bcj->bij', th, ph)
        a = jax.nn.softmax(f, axis=-1)
        y = jnp.einsum('bij,bcj->bci', a, g)
        y = y.reshape(b, -1, h, w)
        return conv1x1(y, Wo, bo) + x

    def _L1_attn_ref(x, W_attn, W_proj):
        import jax, jax.numpy as jnp
        import numpy as np
        N_HEAD = 4
        B, T, C = x.shape
        hs = C // N_HEAD
        qkv = x @ W_attn
        q, k, v = jnp.split(qkv, 3, axis=2)

        def to_heads(t):
            return t.reshape(B, T, N_HEAD, hs).transpose(0, 2, 1, 3)
        q, k, v = (to_heads(q), to_heads(k), to_heads(v))
        scale = 1.0 / np.sqrt(hs).astype(np.float32)
        att = jnp.einsum('bhqd,bhkd->bhqk', q, k) * scale
        causal = jnp.tril(jnp.ones((T, T), dtype=bool))
        att = jnp.where(causal, att, jnp.finfo(att.dtype).min)
        att = jax.nn.softmax(att, axis=-1)
        y = jnp.einsum('bhqk,bhkd->bhqd', att, v)
        y = y.transpose(0, 2, 1, 3).reshape(B, T, C)
        return y @ W_proj

    def _L1_ffn_ref(x, Wr, br, W1, b1, g1, be1, m1, v1, W2, b2, g2, be2, m2, v2, Wo, bo):
        import jax, jax.numpy as jnp
        import numpy as np
        BN_EPS = 0.001

        def _bn(h, g, b, m, v):
            return g * (h - m) * jax.lax.rsqrt(v + BN_EPS) + b
        feat = jnp.mean(x, axis=0)
        w = jax.nn.softmax(feat @ Wr + br, axis=-1)
        h = jnp.einsum('bfd,edh->bfeh', x, W1) + b1
        h = jax.nn.relu(_bn(h, g1, be1, m1, v1))
        h = jnp.einsum('bfeh,ehk->bfek', h, W2) + b2
        h = jax.nn.relu(_bn(h, g2, be2, m2, v2))
        y = jnp.einsum('bfeh,ehd->bfed', h, Wo) + bo
        return jnp.einsum('bfed,fe->bfd', y, w)

    def _gn(v, G=32, eps=1e-05):
        B_, C_, H_, W_ = v.shape
        g = v.reshape(B_, G, C_ // G, H_, W_)
        m = jnp.mean(g, axis=(2, 3, 4), keepdims=True)
        s = jnp.var(g, axis=(2, 3, 4), keepdims=True)
        return ((g - m) / jnp.sqrt(s + eps)).reshape(v.shape)

    def _ln_c(v, eps=1e-06):
        m = jnp.mean(v, axis=1, keepdims=True)
        s = jnp.var(v, axis=1, keepdims=True)
        return (v - m) / jnp.sqrt(s + eps)

    def _ln_t(v, eps=1e-05):
        m = jnp.mean(v, axis=-1, keepdims=True)
        s = jnp.var(v, axis=-1, keepdims=True)
        return (v - m) / jnp.sqrt(s + eps)

    def _to_tokens(v):
        B_, C_, H_, W_ = v.shape
        return v.reshape(B_, C_, H_ * W_).transpose(0, 2, 1)

    def _from_tokens(t, like):
        B_, C_, H_, W_ = like.shape
        return t.transpose(0, 2, 1).reshape(B_, C_, H_, W_)
    x = _L0_conv_ref(x, L0_conv_Wg, L0_conv_bg, L0_conv_Wt, L0_conv_bt, L0_conv_Wp, L0_conv_bp, L0_conv_Wo, L0_conv_bo)
    t = _to_tokens(x)
    t = t + _L1_attn_ref(_ln_t(t), L1_attn_W_attn, L1_attn_W_proj)
    t = t + _L1_ffn_ref(_ln_t(t), L1_ffn_Wr, L1_ffn_br, L1_ffn_W1, L1_ffn_b1, L1_ffn_g1, L1_ffn_be1, L1_ffn_m1, L1_ffn_v1, L1_ffn_W2, L1_ffn_b2, L1_ffn_g2, L1_ffn_be2, L1_ffn_m2, L1_ffn_v2, L1_ffn_Wo, L1_ffn_bo)
    x = _from_tokens(t, x)
    return x

_drawn_inputs = setup_inputs


def setup_inputs(seed=0):
    import zlib

    import numpy as np

    out = dict(_drawn_inputs(seed))
    spreads = {'L0_conv_bg': (0.0, 0.598),
     'L0_conv_bt': (0.0, 0.8),
     'L0_conv_bp': (0.0, 0.8),
     'L0_conv_bo': (0.0, 0.1),
     'L1_ffn_br': (0.0, 0.514),
     'L1_ffn_b1': (0.0, 0.403),
     'L1_ffn_g1': (1.0, 0.2),
     'L1_ffn_be1': (0.0, 0.376),
     'L1_ffn_m1': (0.0, 0.403),
     'L1_ffn_v1': (1.0, 0.6),
     'L1_ffn_b2': (0.0, 0.1),
     'L1_ffn_g2': (1.0, 0.2),
     'L1_ffn_be2': (0.0, 0.309),
     'L1_ffn_m2': (0.0, 0.282),
     'L1_ffn_v2': (1.0, 0.6),
     'L1_ffn_bo': (0.0, 0.1)}
    factors = {'L0_conv_Wg': 8.0, 'L0_conv_Wt': 8.0, 'L0_conv_Wp': 8.0, 'L0_conv_Wo': 4.171}
    for name, (base, spread) in spreads.items():
        noise = np.random.default_rng([zlib.crc32(name.encode()), seed]).standard_normal(out[name].shape)
        drawn = base * np.exp(spread * noise) if base else spread * noise
        out[name] = jnp.asarray(drawn.astype(out[name].dtype))
    for name, factor in factors.items():
        out[name] = (out[name] * factor).astype(out[name].dtype)
    return out
```

```python
from contextlib import ExitStack

import numpy as np

import concourse.bass as bass
from concourse import mybir

F32 = mybir.dt.float32
F32R = mybir.dt.float32r
BF16 = mybir.dt.bfloat16
ALU = mybir.AluOpType
ACT = mybir.ActivationFunctionType
X = mybir.AxisListType.X

P = 128
MASKED = -3.0e38
EPS_LN = 1e-5
EPS_BN = 1e-3

C_IDENT, C_CAUSAL, C_ROLES, C_END = 0, 128, 256, 260
ROLE_THETA, ROLE_PHI, ROLE_Q, ROLE_K = range(4)


def shape_constants():
    c = np.zeros((P, C_END), np.float32)
    p = np.arange(P)
    c[:, C_IDENT:C_IDENT + P] = np.eye(P)
    c[:, C_CAUSAL:C_CAUSAL + P] = np.where(p[None, :] > p[:, None], MASKED, 0.0)
    c[:, C_ROLES + ROLE_THETA] = -((p // 32) % 2)
    c[:, C_ROLES + ROLE_PHI] = -((p // 64) % 2)
    c[:, C_ROLES + ROLE_Q] = -((p // 16) % 2)
    c[:, C_ROLES + ROLE_K] = -((p // 32) % 2)
    return c


def conv_attention_moe(nc, a):
    B, C, H, W = a["x"].shape
    N = H * W
    CI = a["L0_conv_Wg"].shape[0]
    NB = N // P
    HEADS, HS = 4, C // 4
    E = a["L1_ffn_W1"].shape[0]
    PAIRS = E * C // P
    assert (B, C, N, CI, NB, E, PAIRS) == (4, 64, 256, 32, 2, 8, 4)
    SB = 2
    VW = HS + 1
    CX = 2 * C + 1

    with ExitStack() as ctx:
        def sb(name, shape, dt=F32):
            return ctx.enter_context(nc.sbuf_tensor(name, shape, dt))

        def ps(name, shape):
            return ctx.enter_context(nc.psum_tensor(name, shape, F32))

        def sem(name):
            return ctx.enter_context(nc.semaphore(name))

        const = sb("const", [P, C_END])
        ident = const[:, C_IDENT:C_IDENT + P]
        role = [const[:, C_ROLES + i:C_ROLES + i + 1] for i in range(4)]
        neg_ident = sb("neg_ident", [P, P])
        ident_bf = sb("ident_bf", [P, P], BF16)
        causal_bf = sb("causal_bf", [P, P], BF16)
        ones_r = sb("ones_r", [P, P], F32R)
        ones_f = sb("ones_f", [P, P])
        conv_w = sb("conv_w", [CI, 3, C + 1])
        conv_wo = sb("conv_wo", [C, CI])
        conv_woT = sb("conv_woT", [CI, C])
        conv_th4 = sb("conv_th4", [C + 1, 2, P])
        conv_vx = sb("conv_vx", [C + 1, CX])
        attn_w = sb("attn_w", [P, 3 * C])
        attn_qk = sb("attn_qk", [P, 2, HEADS, HS])
        attn_qk_hi = sb("attn_qk_hi", [P, 2, HEADS, 4, HS], F32R)
        attn_qk_lo = sb("attn_qk_lo", [P, 2, HEADS, 4, HS], F32R)
        attn_v_hi = sb("attn_v_hi", [P, C], F32R)
        attn_v_lo = sb("attn_v_lo", [P, C], F32R)
        attn_proj = sb("attn_proj", [C, C])
        w1 = sb("w1", [P, E, C])
        w1_hi = sb("w1_hi", [P, E * C], F32R)
        w1_lo = sb("w1_lo", [P, E * C], F32R)
        w2 = sb("w2", [P, PAIRS, P])
        w2s = sb("w2s", [P, PAIRS, P])
        wo = sb("wo", [P, PAIRS, C])
        bn_rows = sb("bn_rows", [2 * 5 * PAIRS, P])
        bn = sb("bn", [P, 2, 5, PAIRS])
        bn_var = sb("bn_var", [P, 2, PAIRS])
        bn_rs = sb("bn_rs", [P, 2, PAIRS])
        bn_s = sb("bn_s", [P, 2, PAIRS])
        bn_d = sb("bn_d", [P, 2, PAIRS])
        bn_ds = sb("bn_ds", [P, 2, PAIRS])
        bn_c = sb("bn_c", [P, 2, PAIRS])
        bn_nc = sb("bn_nc", [P, PAIRS])
        s2_diag = sb("s2_diag", [P, PAIRS, P])
        c2_blk = sb("c2_blk", [P, PAIRS * E])
        wr = sb("wr", [P, E])
        wr4 = sb("wr4", [P, E])
        br = sb("br", [1, E])
        bo = sb("bo", [E, C])
        cmat = sb("cmat", [E, C])
        pair_sel = sb("pair_sel", [E, E, C])
        half = sb("half", [P, 2 * PAIRS])

        def per_batch(name, shape, dt=F32):
            return [sb(f"{name}{b}", shape, dt) for b in range(B)]

        x1 = sb("x1", [C + 1, B, N])
        f_tmp = per_batch("f_tmp", [P, 2, N], F32R)
        th_s = per_batch("th_s", [P, N], F32R)
        ph_s = per_batch("ph_s", [P, N], F32R)
        vx = per_batch("vx", [P, NB, CX])
        m1 = per_batch("m1", [P, NB])
        diag1 = per_batch("diag1", [P, NB, P], F32R)
        p1 = per_batch("p1", [P, NB, N])
        r1 = per_batch("r1", [P, NB])
        t1 = per_batch("t1", [P, NB, C])
        t2 = per_batch("t2", [P, NB, C])
        ln = [dict(st=per_batch(f"ln{i}_st", [P, NB, 6]), mv=per_batch(f"ln{i}_mv", [P, NB, 2]),
                   var=per_batch(f"ln{i}_var", [P, NB]), rs=per_batch(f"ln{i}_rs", [P, NB]),
                   xh=per_batch(f"ln{i}_xh", [P, NB, C]), xs=per_batch(f"ln{i}_xs", [P, NB, 2, C]))
              for i in range(2)]
        xT = per_batch("xT", [P, N], F32R)
        x2T = sb("x2T", [P, B, N], F32R)
        qk_tmp = per_batch("qk_tmp", [P, 2, 2 * N], F32R)
        q_s = per_batch("q_s", [P, 2, N], F32R)
        k_s = per_batch("k_s", [P, 2, N], F32R)
        v2 = per_batch("v2", [P, NB, HEADS, VW])
        m2 = per_batch("m2", [P, NB, HEADS])
        diag2 = per_batch("diag2", [P, HEADS, NB, P], F32R)
        p2 = per_batch("p2", [P, 3, 512])
        r2 = per_batch("r2", [P, NB * HEADS])
        y2 = per_batch("y2", [P, NB, C])
        yT = per_batch("yT", [C, N])
        h1 = sb("h1", [P, PAIRS, B * N])
        xsum = [sb(f"xsum{i}", [P, N]) for i in range(B - 1)]
        gm = sb("gm", [P, NB])
        gl = sb("gl", [P, NB, E])
        ge = sb("ge", [P, NB, E])
        gs = sb("gs", [P, NB])
        gr = sb("gr", [P, NB])
        gw = sb("gw", [P, NB, E])
        gwT = sb("gwT", [E, N])
        w_b = sb("w_b", [P, PAIRS, N])
        cw = sb("cw", [C, N])
        h2 = [sb(f"h2_{i}", [P, SB, N]) for i in range(4)]
        o_sb = [sb(f"o_sb{i}", [C, SB, N]) for i in range(B // SB)]

        A = ps("A", [P, 3, 512])
        PR = [ps(f"PR{i}", [P, 512]) for i in range(2)]
        Q = [ps(f"Q{i}", [P, 512]) for i in range(2)]
        M = ps("M", [P, 512])
        pv1 = M[:, 0:NB * (C + 1)].rearrange("p (n c) -> p n c", n=NB)
        vps = M[:, 130:130 + NB * C]
        pv2 = M[:, 258:258 + NB * HEADS * VW].rearrange("p (n c) -> p n c", c=VW)

        x_in = [sem(f"x_in{b}") for b in range(B)]
        const_in, convw_in, attnw_in, bn_in, ffnw_in, out_done = map(
            sem, ("const_in", "convw_in", "attnw_in", "bn_in", "ffnw_in", "out_done"))
        x_ones = sem("x_ones")
        filled = sem("filled")
        v_const = sem("v_const")
        conv_T, woT_ok, vx_w, th4_ok, vxw_ok = map(sem, ("conv_T", "woT_ok", "vx_w", "th4_ok", "vxw_ok"))
        aw_scaled, aw_hi, aw_ok = map(sem, ("aw_scaled", "aw_hi", "aw_ok"))
        w1_rounded, w1_ok = sem("w1_rounded"), sem("w1_ok")
        bn_T, bn_ok, bn_step, bn_pow, s2d_ok, s2_b, w2s_ok = map(
            sem, ("bn_T", "bn_ok", "bn_step", "bn_pow", "s2d_ok", "s2_b", "w2s_ok"))
        c2_ok, cm_ps, cm_ok, wr_ok, sel_ok = map(sem, ("c2_ok", "cm_ps", "cm_ok", "wr_ok", "sel_ok"))
        f_ps, vx_ps, f_rnd, f_split, vx_ok = map(sem, ("f_ps", "vx_ps", "f_rnd", "f_split", "vx_ok"))
        s1_ps, m1_ok, d1_ok, s1t_ps, p1_ok, pv1_ps, r1_ok, t1_ok = map(
            sem, ("s1_ps", "m1_ok", "d1_ok", "s1t_ps", "p1_ok", "pv1_ps", "r1_ok", "t1_ok"))
        for i, l in enumerate(ln):
            for n in ("stats", "aggr", "eps", "pow", "xh", "hi", "xs", "T", "TT"):
                l["s_" + n] = sem(f"ln{i}_s_{n}")
        q_ps, k_ps, v_ps, q_rnd, k_rnd, q_ok, k_ok, v_ok = map(
            sem, ("q_ps", "k_ps", "v_ps", "q_rnd", "k_rnd", "q_ok", "k_ok", "v_ok"))
        s2a_ps, s2b_ps, m2_ok, d2_ok, s2t_ps, p2_ok = map(
            sem, ("s2a_ps", "s2b_ps", "m2_ok", "d2_ok", "s2t_ps", "p2_ok"))
        pv2_ps, r2_ok, y_ok, yT_ps, yT_ok, pj_ps, t2_ok = map(
            sem, ("pv2_ps", "r2_ok", "y_ok", "yT_ps", "yT_ok", "pj_ps", "t2_ok"))
        rows_done = sem("rows_done")
        l1_ps, h1_ok, xsum_ok = map(sem, ("l1_ps", "h1_ok", "xsum_ok"))
        g_ps, g_step, g_exp, g_ok, gT_ps, gT_ok, wb_ps, wb_ok, cw_ps, cw_ok = map(
            sem, ("g_ps", "g_step", "g_exp", "g_ok", "gT_ps", "gT_ok", "wb_ps", "wb_ok", "cw_ps", "cw_ok"))
        l2_ps, h2_ok, l3_step, l3_ps, o_ok = map(sem, ("l2_ps", "h2_ok", "l3_step", "l3_ps", "o_ok"))

        STEPS, LAG = 13, 2

        def schedule():
            for s in range(STEPS + LAG * (B - 1)):
                for b in range(B):
                    if 0 <= s - LAG * b < STEPS:
                        yield s - LAG * b, b

        N_CONVW, N_ATTNW, N_BN, N_FFNW = 8, 3, 10, 9

        block = ctx.enter_context(nc.Block())

        @block.sync
        def _(sp):
            def load(dst, src, s):
                sp.dma_start(dst, src).then_inc(s, 16)

            xv = a["x"].rearrange("b c h w -> b c (h w)")
            for i, n in enumerate(("t", "p", "g")):
                load(conv_w[:, i, 0:C], a[f"L0_conv_W{n}"], convw_in)
            load(conv_wo[:, :], a["L0_conv_Wo"], convw_in)
            load(x1[0:C, 0, :], xv[0], x_in[0])
            load(x1[0:C, 1, :], xv[1], x_in[1])
            load(attn_w[0:C, :], a["L1_attn_W_attn"], attnw_in)
            load(attn_w[C:P, :], a["L1_attn_W_attn"], attnw_in)
            load(x1[0:C, 2, :], xv[2], x_in[2])
            load(x1[0:C, 3, :], xv[3], x_in[3])
            load(attn_proj[:, :], a["L1_attn_W_proj"], attnw_in)
            for i in range(2):
                for j, n in enumerate(("g", "b", "m", "v", "be")):
                    r = (5 * i + j) * PAIRS
                    load(bn_rows[r:r + PAIRS, :],
                         a[f"L1_ffn_{n}{i + 1}"].rearrange("e h -> (e h)").rearrange("(q p) -> q p", p=P), bn_in)
            w1_v = a["L1_ffn_W1"].rearrange("e d h -> d e h")
            load(w1[0:C, :, :], w1_v, ffnw_in)
            load(w1[C:P, :, :], w1_v, ffnw_in)
            sp.wait_ge(filled, 1)
            w2_v = a["L1_ffn_W2"].rearrange("(q t) h k -> t h q k", t=2)
            for t in range(2):
                load(w2[C * t:C * t + C, :, C * t:C * t + C], w2_v[t], ffnw_in)
            load(wo[:, :, :], a["L1_ffn_Wo"].rearrange("e h d -> (e h) d").rearrange("(q p) d -> p q d", p=P), ffnw_in)
            load(wr[0:C, :], a["L1_ffn_Wr"], ffnw_in)
            load(wr[C:P, :], a["L1_ffn_Wr"], ffnw_in)
            load(br[:, :], a["L1_ffn_br"].rearrange("(a e) -> a e", a=1), ffnw_in)
            load(bo[:, :], a["L1_ffn_bo"], ffnw_in)
            ov = a["out"].rearrange("b c h w -> b c (h w)").rearrange("b c n -> c b n")
            for s in range(B // SB):
                sp.wait_ge(o_ok, s + 1)
                sp.dma_start(ov[:, SB * s:SB * s + SB, :], o_sb[s][:, :, :]).then_inc(out_done, 16)
            sp.wait_ge(out_done, 16 * (B // SB))

        @block.gpsimd
        def _(pool):
            pool.memset(w2[:, :, :], 0.0).then_inc(filled, 1)
            pool.memset(ones_f[:, :], 1.0).then_inc(filled, 1)
            pool.memset(half[:, :], -0.5).then_inc(filled, 1)
            pool.memset(c2_blk[:, :], 0.0).then_inc(filled, 1)
            for b in range(B):
                pool.memset(v2[b][:, :, :, :], 1.0).then_inc(filled, 1)

            def diagonal(out, m, batch_dims):
                n = m.shape[1]
                return pool.tensor_tensor(out, neg_ident[:, :].unsqueeze(1).to_broadcast([P, n, P]),
                                          m.unsqueeze(2).to_broadcast([P, n, P]), ALU.mult)

            def root(i, b):
                pool.wait_ge(ln[i]["s_eps"], b + 1)
                pool.tensor_tensor(ln[i]["rs"][b][:, :], ln[i]["var"][b][:, :], half[:, 0:NB],
                                   ALU.pow).then_inc(ln[i]["s_pow"], 1)

            for step, b in schedule():
                if step == 1:
                    if b == 0:
                        pool.wait_ge(v_const, 3)
                        pool.wait_ge(filled, 3)
                    pool.wait_ge(m1_ok, b + 1)
                    diagonal(diag1[b][:, :, :], m1[b][:, :], 1).then_inc(d1_ok, 1)
                if step == 3:
                    root(0, b)
                    if b == 0:
                        pool.wait_ge(bn_step, 1)
                        pool.tensor_tensor(bn_rs[:, :, :].rearrange("p a q -> p (a q)"),
                                           bn_var[:, :, :].rearrange("p a q -> p (a q)"), half[:, :],
                                           ALU.pow).then_inc(bn_pow, 1)
                        pool.wait_ge(bn_step, 3)
                        pool.tensor_tensor(s2_diag[:, :, :], ident.unsqueeze(1).to_broadcast([P, PAIRS, P]),
                                           bn_s[:, 1, :].unsqueeze(2).to_broadcast([P, PAIRS, P]),
                                           ALU.mult).then_inc(s2d_ok, 1)
                if step == 6:
                    for i in range(NB):
                        pool.wait_ge(m2_ok, NB * b + i + 1)
                        diagonal(diag2[b][:, :, i, :], m2[b][:, i, :], 1).then_inc(d2_ok, 1)
                if step == 10:
                    root(1, b)
                if step == 11 and b > 0:
                    pool.wait_ge(ln[1]["s_TT"], b + 1)
                    if b > 1:
                        pool.wait_ge(xsum_ok, b - 1)
                    first = (x2T[:, 0, :].bitcast(F32) if b == 1 else xsum[b - 2][:, :])
                    pool.tensor_tensor(xsum[b - 1][:, :], first, x2T[:, b, :].bitcast(F32),
                                       ALU.add).then_inc(xsum_ok, 1)

        @block.scalar
        def _(act):
            act.dma_start(const[:, :], a["constants"]).then_inc(const_in, 16)
            for i, n in enumerate(("t", "p", "g")):
                act.dma_start(conv_w[:, i, C:C + 1],
                              a[f"L0_conv_b{n}"].rearrange("(c a) -> c a", a=1)).then_inc(convw_in, 16)
            act.dma_start(conv_vx[C:C + 1, C + 1:CX],
                          a["L0_conv_bo"].rearrange("(a c) -> a c", a=1)).then_inc(convw_in, 16)

            def copy(out, in_):
                return act.activation(out, in_, ACT.Copy)

            act.wait_ge(conv_T, 1)
            copy(conv_th4[:, :, :], Q[0][0:C + 1, 0:2 * P].rearrange("c (t p) -> c t p", t=2)).then_inc(th4_ok, 1)
            act.wait_ge(vx_w, 1)
            copy(conv_vx[:, 0:C], Q[1][0:C + 1, C:2 * C]).then_inc(vxw_ok, 1)

            def xT_copy(i, b, out, bank):
                act.wait_ge(ln[i]["s_T"], b + 1)
                copy(out, bank[:, 0:N]).then_inc(ln[i]["s_TT"], 1)

            for step, b in schedule():
                if step == 0:
                    act.wait_ge(f_ps, b + 1)
                    copy(f_tmp[b][:, :, :], Q[b % 2][:, :].rearrange("p (t n) -> p t n", t=2)).then_inc(f_rnd, 1)
                    act.wait_ge(vx_ps, b + 1)
                    copy(vx[b][:, :, :], PR[0][:, 0:NB * CX].rearrange("p (n c) -> p n c", n=NB)).then_inc(vx_ok, 1)
                if step == 2:
                    act.wait_ge(s1t_ps, b + 1)
                    act.activation(p1[b][:, :, :], Q[b % 2][:, :].rearrange("p (n i) -> p n i", n=NB),
                                   ACT.Exp).then_inc(p1_ok, 1)
                    if b == 0:
                        act.wait_ge(bn_T, 1)
                        copy(bn[:, :, :, :], A[:, 0, 0:10 * PAIRS].rearrange("p (a v q) -> p a v q", a=2, v=5))\
                            .then_inc(bn_ok, 1)
                if step == 4:
                    xT_copy(0, b, xT[b][:, :], PR[1])
                    if b == 0:
                        act.wait_ge(cm_ps, 1)
                        copy(cmat[:, :], A[0:E, 2, 0:C]).then_inc(cm_ok, 1)
                if step == 5:
                    act.wait_ge(v_ps, b + 1)
                    act.wait_ge(filled, 5 + b)
                    copy(v2[b][:, :, :, 0:HS], vps.rearrange("p (n h d) -> p n h d", n=NB, h=HEADS)).then_inc(v_ok, 1)
                    act.wait_ge(q_ps, b + 1)
                    copy(qk_tmp[b][:, 0, :], PR[0][:, :]).then_inc(q_rnd, 1)
                    act.wait_ge(k_ps, b + 1)
                    copy(qk_tmp[b][:, 1, :], PR[1][:, :]).then_inc(k_rnd, 1)
                if step == 7:
                    act.wait_ge(s2t_ps, b + 1)
                    act.activation(p2[b][:, :, :], A[:, :, :], ACT.Exp).then_inc(p2_ok, 1)
                if step == 9:
                    act.wait_ge(yT_ps, b + 1)
                    copy(yT[b][:, :], Q[0][0:C, 0:N]).then_inc(yT_ok, 1)
                if step == 11:
                    xT_copy(1, b, x2T[:, b, :], Q[1])
                if step == 12 and b % SB == SB - 1:
                    s = b // SB
                    if s == 0:
                        act.wait_ge(bn_step, 6)
                    for q in range(PAIRS):
                        n = PAIRS * s + q
                        act.wait_ge(l1_ps, n + 1)
                        act.activation(h1[:, q, SB * N * s:SB * N * (s + 1)], PR[n % 2][:, :], ACT.Relu,
                                       bias=bn_c[:, 0, q:q + 1], scale=bn_s[:, 0, q:q + 1]).then_inc(h1_ok, 1)
            act.wait_ge(g_step, 2)
            act.activation(ge[:, :, :], gl[:, :, :], ACT.Exp).then_inc(g_exp, 1)
            act.wait_ge(gT_ps, 1)
            copy(gwT[:, :], M[0:E, N:2 * N]).then_inc(gT_ok, 1)
            for i in range(2):
                act.wait_ge(wb_ps, i + 1)
                copy(w_b[:, 2 * i:2 * i + 2, :], A[:, i, :].rearrange("p (q n) -> p q n", q=2)).then_inc(wb_ok, 1)
            act.wait_ge(cw_ps, 1)
            copy(cw[:, :], M[0:C, 0:N]).then_inc(cw_ok, 1)

        @block.vector
        def _(v):
            def mul_add(out, in0, scalar, in1):
                return v.scalar_tensor_tensor(out=out, in0=in0, scalar=scalar, in1=in1, op0=ALU.mult, op1=ALU.add)

            v.memset(x1[C:C + 1, :, :], 1.0).then_inc(x_ones, 1)
            v.memset(ones_r[:, :].bitcast(F32), 1.0).then_inc(v_const, 1)
            v.wait_ge(const_in, 16)
            v.tensor_copy(conv_vx[0:C, C + 1:CX], ident[0:C, 0:C]).then_inc(v_const, 1)
            v.tensor_scalar(neg_ident[:, :], ident, -1.0, None, ALU.mult).then_inc(v_const, 1)
            v.tensor_copy(conv_vx[:, C:C + 1], ident[0:C + 1, C:C + 1]).then_inc(v_const, 1)
            v.tensor_copy(ident_bf[:, :], ident).then_inc(v_const, 1)
            v.tensor_copy(causal_bf[:, :], const[:, C_CAUSAL:C_CAUSAL + P]).then_inc(v_const, 1)
            v.tensor_copy(pair_sel[:, :, :], ident[0:E, 0:E].unsqueeze(2).to_broadcast([E, E, C])).then_inc(sel_ok, 1)
            v.wait_ge(conv_T, 2)
            v.tensor_copy(conv_woT[:, :], Q[1][0:CI, 0:C]).then_inc(woT_ok, 1)

            def attention_weights():
                v.wait_ge(attnw_in, 16 * N_ATTNW)
                v.tensor_scalar(attn_qk[:, 0, :, :], attn_w[:, 0:C].rearrange("p (h d) -> p h d", h=HEADS),
                                float(HS) ** -0.5, None, ALU.mult).then_inc(aw_scaled, 1)
                v.tensor_copy(attn_qk[:, 1, :, :], attn_w[:, C:2 * C].rearrange("p (h d) -> p h d", h=HEADS))\
                    .then_inc(aw_scaled, 1)
                v.tensor_copy(attn_v_hi[:, :], attn_w[:, 2 * C:3 * C]).then_inc(aw_hi, 1)
                v.wait_ge(aw_scaled, 2)
                four = [attn_qk[:, i, :, :].unsqueeze(2).to_broadcast([P, HEADS, 4, HS]) for i in range(2)]
                for i in range(2):
                    v.tensor_copy(attn_qk_hi[:, i, :, :, :], four[i]).then_inc(aw_hi, 1)
                v.wait_ge(aw_hi, 3)
                for i in range(2):
                    v.tensor_tensor(attn_qk_lo[:, i, :, :, :], four[i], attn_qk_hi[:, i, :, :, :].bitcast(F32),
                                    ALU.subtract).then_inc(aw_ok, 1)
                v.tensor_tensor(attn_v_lo[:, :], attn_w[:, 2 * C:3 * C], attn_v_hi[:, :].bitcast(F32),
                                ALU.subtract).then_inc(aw_ok, 1)

            def norm_parameters(part):
                g, bb, m, var, be = (bn[:, :, j, :] for j in range(5))
                if part == 0:
                    v.wait_ge(bn_ok, 1)
                    v.tensor_scalar(bn_var[:, :, :], var, EPS_BN, None, ALU.add).then_inc(bn_step, 1)
                    v.tensor_tensor(bn_d[:, :, :], bb, m, ALU.subtract).then_inc(bn_step, 1)
                    return
                v.wait_ge(bn_pow, 1)
                v.tensor_tensor(bn_s[:, :, :], g, bn_rs[:, :, :], ALU.mult).then_inc(bn_step, 1)
                v.wait_ge(bn_step, 3)
                v.tensor_tensor(bn_ds[:, :, :], bn_d[:, :, :], bn_s[:, :, :], ALU.mult).then_inc(bn_step, 1)
                v.wait_ge(bn_step, 4)
                v.tensor_tensor(bn_c[:, :, :], bn_ds[:, :, :], be, ALU.add).then_inc(bn_step, 1)
                v.wait_ge(bn_step, 5)
                v.tensor_scalar(bn_nc[:, :], bn_c[:, 1, :], -1.0, None, ALU.mult).then_inc(bn_step, 1)
                v.wait_ge(filled, 4)
                for t in range(2):
                    v.tensor_copy(c2_blk[C * t:C * t + C, t:t + (E + 2) * (PAIRS - 1) + 1:E + 2],
                                  bn_c[C * t:C * t + C, 1, :]).then_inc(c2_ok, 1)

            def expert_weights():
                v.wait_ge(ffnw_in, 16 * N_FFNW)
                w1f = w1[:, :, :].rearrange("p e h -> p (e h)")
                v.tensor_copy(w1_hi[:, :], w1f).then_inc(w1_rounded, 1)
                v.tensor_scalar(wr4[:, :], wr[:, :], 1.0 / B, None, ALU.mult).then_inc(wr_ok, 1)
                v.wait_ge(w1_rounded, 1)
                v.tensor_tensor(w1_lo[:, :], w1f, w1_hi[:, :].bitcast(F32), ALU.subtract).then_inc(w1_ok, 1)

            def layer_norm(i, b, t, ready):
                l = ln[i]
                v.wait_ge(ready, b + 1)
                for n in range(NB):
                    v.bn_stats(l["st"][b][:, n, :], t[:, n, :]).then_inc(l["s_stats"], 1)
                for n in range(NB):
                    v.wait_ge(l["s_stats"], NB * b + n + 1)
                    v.bn_aggr(l["mv"][b][:, n, :], l["st"][b][:, n, :]).then_inc(l["s_aggr"], 1)
                v.wait_ge(l["s_aggr"], NB * (b + 1))
                v.tensor_scalar(l["var"][b][:, :], l["mv"][b][:, :, 1], EPS_LN, None, ALU.add).then_inc(l["s_eps"], 1)

            def normed(i, b, t):
                l = ln[i]
                v.wait_ge(l["s_pow"], b + 1)
                for n in range(NB):
                    v.tensor_scalar(l["xh"][b][:, n, :], t[:, n, :], l["mv"][b][:, n, 0:1], l["rs"][b][:, n:n + 1],
                                    ALU.subtract, ALU.mult).then_inc(l["s_xh"], 1)
                v.wait_ge(l["s_xh"], NB * (b + 1))
                v.tensor_copy(l["xs"][b][:, :, 0, :].bitcast(F32R), l["xh"][b][:, :, :]).then_inc(l["s_hi"], 1)
                v.wait_ge(l["s_hi"], b + 1)
                v.tensor_tensor(l["xs"][b][:, :, 1, :], l["xh"][b][:, :, :], l["xs"][b][:, :, 0, :],
                                ALU.subtract).then_inc(l["s_xs"], 1)

            for step, b in schedule():
                if step == 0:
                    v.wait_ge(f_rnd, b + 1)
                    for i, (out, r) in enumerate(((th_s, ROLE_THETA), (ph_s, ROLE_PHI))):
                        mul_add(out[b][:, :], f_tmp[b][:, i, :].bitcast(F32), role[r],
                                Q[b % 2][:, i * N:(i + 1) * N]).then_inc(f_split, 1)
                    if b == 0:
                        attention_weights()
                if step == 1:
                    v.wait_ge(s1_ps, b + 1)
                    v.tensor_reduce(m1[b][:, :], Q[(b + 1) % 2][:, :].rearrange("p (n j) -> p n j", n=NB), X,
                                    ALU.max).then_inc(m1_ok, 1)
                if step == 2 and b == 0:
                    norm_parameters(0)
                    expert_weights()
                if step == 3:
                    v.wait_ge(pv1_ps, b + 1)
                    v.reciprocal(r1[b][:, :], pv1[:, :, C]).then_inc(r1_ok, 1)
                    v.wait_ge(r1_ok, b + 1)
                    v.wait_ge(vx_ok, b + 1)
                    for n in range(NB):
                        i = mul_add(t1[b][:, n, :], pv1[:, n, 0:C], r1[b][:, n:n + 1], vx[b][:, n, C + 1:CX])
                    i.then_inc(t1_ok, 1)
                    layer_norm(0, b, t1[b], t1_ok)
                    if b == 0:
                        norm_parameters(1)
                    normed(0, b, t1[b])
                if step == 4 and b == 0:
                    v.wait_ge(s2_b, 1)
                    v.tensor_tensor(w2s[:, :, :], w2[:, :, :], A[:, 1, :].rearrange("p (q k) -> p q k", q=PAIRS),
                                    ALU.mult).then_inc(w2s_ok, 1)
                if step == 5:
                    for i, (out, r, rnd, ok) in enumerate(((q_s, ROLE_Q, q_rnd, q_ok), (k_s, ROLE_K, k_rnd, k_ok))):
                        v.wait_ge(rnd, b + 1)
                        mul_add(out[b][:, :, :].rearrange("p g n -> p (g n)"), qk_tmp[b][:, i, :].bitcast(F32),
                                role[r], PR[i][:, :]).then_inc(ok, 1)
                if step == 6:
                    v.wait_ge(s2a_ps, b + 1)
                    v.tensor_reduce(m2[b][:, 0, :], A[:, 0, :].rearrange("p (h j) -> p h j", h=HEADS), X,
                                    ALU.max).then_inc(m2_ok, 1)
                    v.wait_ge(s2b_ps, 2 * (b + 1))
                    v.tensor_reduce(m2[b][:, 1, :].rearrange("p (g t) -> p t g", t=2),
                                    A[:, 1:3, :].rearrange("p t (g j) -> p t g j", g=2), X,
                                    ALU.max).then_inc(m2_ok, 1)
                if step == 8:
                    v.wait_ge(pv2_ps, b + 1)
                    v.reciprocal(r2[b][:, :], pv2[:, :, HS]).then_inc(r2_ok, 1)
                    v.wait_ge(r2_ok, b + 1)
                    v.tensor_tensor(y2[b][:, :, :].rearrange("p n (h d) -> p (n h) d", h=HEADS), pv2[:, :, 0:HS],
                                    r2[b][:, :].unsqueeze(2).to_broadcast([P, NB * HEADS, HS]),
                                    ALU.mult).then_inc(y_ok, 1)
                if step == 10:
                    v.wait_ge(pj_ps, b + 1)
                    v.tensor_tensor(t2[b][:, :, :], Q[0][:, N:N + NB * C].rearrange("p (n c) -> p n c", n=NB),
                                    t1[b][:, :, :], ALU.add).then_inc(t2_ok, 1)
                    layer_norm(1, b, t2[b], t2_ok)
                    normed(1, b, t2[b])
            v.wait_ge(g_ps, 1)
            logits = M[:, 0:NB * E].rearrange("p (n e) -> p n e", n=NB)
            v.tensor_reduce(gm[:, :], logits, X, ALU.max).then_inc(g_step, 1)
            v.wait_ge(g_step, 1)
            v.tensor_tensor(gl[:, :, :], logits, gm[:, :].unsqueeze(2).to_broadcast([P, NB, E]),
                            ALU.subtract).then_inc(g_step, 1)
            v.wait_ge(g_exp, 1)
            v.tensor_reduce(gs[:, :], ge[:, :, :], X, ALU.add).then_inc(g_step, 1)
            v.wait_ge(g_step, 3)
            v.reciprocal(gr[:, :], gs[:, :]).then_inc(g_step, 1)
            v.wait_ge(g_step, 4)
            v.tensor_tensor(gw[:, :, :], ge[:, :, :], gr[:, :].unsqueeze(2).to_broadcast([P, NB, E]),
                            ALU.mult).then_inc(g_ok, 1)
            ring = [Q[0], Q[1], PR[0], PR[1]]
            for s in range(B // SB):
                for q in range(PAIRS):
                    n = PAIRS * s + q
                    v.wait_ge(l2_ps, n + 1)
                    v.wait_ge(wb_ok, q // 2 + 1)
                    if n >= len(h2):
                        v.wait_ge(l3_step, n - len(h2) + 1)
                    v.scalar_tensor_tensor(out=h2[n % 4][:, :, :], in0=ring[n % 4][:, :].rearrange("p (b n) -> p b n", b=SB),
                                           scalar=bn_nc[:, q:q + 1],
                                           in1=w_b[:, q, :].unsqueeze(1).to_broadcast([P, SB, N]),
                                           op0=ALU.max, op1=ALU.mult).then_inc(h2_ok, 1)
                v.wait_ge(l3_ps, s + 1)
                v.wait_ge(cw_ok, 1)
                v.tensor_tensor(o_sb[s][:, :, :], A[0:C, 2 * (1 - s), :].rearrange("p (b n) -> p b n", b=SB),
                                cw[:, :].unsqueeze(1).to_broadcast([C, SB, N]), ALU.add).then_inc(o_ok, 1)

        @block.tensor
        def _(pe):
            def mm(out, lhsT, rhs, start=True, stop=True, **k):
                return pe.matmul(out, lhsT, rhs, start=start, stop=stop, **k)

            pe.wait_ge(const_in, 16)
            pe.wait_ge(convw_in, 16 * N_CONVW)
            four = ident[0:CI, 0:CI].unsqueeze(1).to_broadcast([CI, 4, CI])
            for i in range(2):
                last = mm(Q[0][0:C + 1, i * P:(i + 1) * P].rearrange("p (r c) -> p r c", r=4), conv_w[:, i, :], four)
            last.then_inc(conv_T, 1)
            pe.transpose(Q[1][0:CI, 0:C], conv_wo[:, :], ident[0:C, 0:C]).then_inc(conv_T, 1)
            pe.wait_ge(woT_ok, 1)
            mm(Q[1][0:C + 1, C:2 * C], conv_w[:, 2, :], conv_woT[:, :]).then_inc(vx_w, 1)

            def transposed(i, b, bank):
                pe.wait_ge(ln[i]["s_xs"], b + 1)
                for n in range(NB):
                    last = pe.transpose(bank[:, n * P:(n + 1) * P],
                                        ln[i]["xs"][b][:, n, :, :].rearrange("p t c -> p (t c)"), ident)
                last.then_inc(ln[i]["s_T"], 1)

            for step, b in schedule():
                if step == 0:
                    pe.wait_ge(x_in[b], 16)
                    if b == 0:
                        pe.wait_ge(x_ones, 1)
                        pe.wait_ge(th4_ok, 1)
                    else:
                        pe.wait_ge(m1_ok, b)
                        pe.wait_ge(vx_ok, b)
                    for i in range(2):
                        last = mm(Q[b % 2][:, i * N:(i + 1) * N], conv_th4[:, i, :], x1[:, b, :])
                    last.then_inc(f_ps, 1)
                    if b == 0:
                        pe.wait_ge(v_const, 4)
                        pe.wait_ge(vxw_ok, 1)
                    if b >= 3:
                        pe.wait_ge(q_ok, b - 2)
                    for n in range(NB):
                        last = mm(PR[0][:, n * CX:(n + 1) * CX], x1[:, b, n * P:(n + 1) * P], conv_vx[:, :])
                    last.then_inc(vx_ps, 1)
                if step == 1:
                    pe.wait_ge(f_split, 2 * (b + 1))
                    if b > 0:
                        pe.wait_ge(p1_ok, b)
                    for n in range(NB):
                        last = mm(Q[(b + 1) % 2][:, n * N:(n + 1) * N], th_s[b][:, n * P:(n + 1) * P], ph_s[b][:, :])
                    last.then_inc(s1_ps, 1)
                    if b == 0:
                        pe.wait_ge(bn_in, 16 * N_BN)
                        pe.transpose(A[:, 0, 0:10 * PAIRS], bn_rows[:, :], ident[0:10 * PAIRS, 0:10 * PAIRS])\
                            .then_inc(bn_T, 1)
                if step == 2:
                    for n in range(NB):
                        out = Q[b % 2][:, n * N:(n + 1) * N]
                        mm(out, ph_s[b][:, n * P:(n + 1) * P], th_s[b][:, :], stop=False)
                        if n == 0:
                            pe.wait_ge(d1_ok, b + 1)
                        last = mm(out, ones_r[:, :], diag1[b][:, :, :].rearrange("p n i -> p (n i)"), start=False)
                    last.then_inc(s1t_ps, 1)
                if step == 3:
                    pe.wait_ge(p1_ok, b + 1)
                    pe.wait_ge(vx_ok, b + 1)
                    if b > 0:
                        pe.wait_ge(v_ok, b)
                    if b > 2:
                        pe.wait_ge(y_ok, b - 2)
                    for i in range(NB):
                        for j in range(NB):
                            last = mm(pv1[:, i, :], p1[b][:, j, i * P:(i + 1) * P], vx[b][:, j, 0:C + 1],
                                      start=(j == 0), stop=(j == NB - 1))
                    last.then_inc(pv1_ps, 1)
                if step == 4:
                    if b > 0:
                        pe.wait_ge(k_ok, b)
                    if b == 0:
                        pe.wait_ge(s2d_ok, 1)
                        pe.wait_ge(filled, 2)
                        mm(A[:, 1, :], ones_f[:, :], s2_diag[:, :, :].rearrange("p q k -> p (q k)")).then_inc(s2_b, 1)
                        pe.wait_ge(c2_ok, 2)
                        pe.wait_ge(ffnw_in, 16 * N_FFNW)
                        for q in range(PAIRS):
                            mm(A[0:E, 2, 0:C], c2_blk[:, q * E:(q + 1) * E], wo[:, q, :], start=(q == 0), stop=False)
                        mm(A[0:E, 2, 0:C], ident[0:E, 0:E], bo[:, :], start=False).then_inc(cm_ps, 1)
                    transposed(0, b, PR[1])
                if step == 5:
                    pe.wait_ge(ln[0]["s_TT"], b + 1)
                    if b == 0:
                        pe.wait_ge(aw_ok, 3)
                    pe.wait_ge(t1_ok, b + 1)
                    if b > 1:
                        pe.wait_ge(y_ok, b - 1)
                    for n in range(NB):
                        for part, w in enumerate((attn_v_hi, attn_v_lo)):
                            last = mm(vps[:, n * C:(n + 1) * C], xT[b][:, n * P:(n + 1) * P], w[:, :],
                                      start=(part == 0), stop=(part == 1))
                    last.then_inc(v_ps, 1)
                    pe.wait_ge(vx_ok, min(b + 3, B))
                    for i, (bank, ps_sem) in enumerate(((PR[0], q_ps), (PR[1], k_ps))):
                        for g in range(2):
                            for part, w in enumerate((attn_qk_hi, attn_qk_lo)):
                                last = mm(bank[:, g * N:(g + 1) * N],
                                          w[:, i, 2 * g:2 * g + 2, :, :].rearrange("p h r d -> p (h r d)"),
                                          xT[b][:, :], start=(part == 0), stop=(part == 1))
                        last.then_inc(ps_sem, 1)

                def rows(s, h, cols):
                    return s[b][64 * (h % 2):64 * (h % 2) + 64, h // 2, cols]

                def masked_pair(out, t, left, right, cols, mask_l, mask_r, start, stop):
                    for g in range(2):
                        mm(out[:, g, :], rows(left, 2 * g + t, cols), rows(right, 2 * g + t, cols),
                           start=(start and g == 0), stop=False)
                    l, r = mask_l[:, :], mask_r[:, :].unsqueeze(1).to_broadcast([P, 2, P])
                    return mm(out, l, r, start=False, stop=stop)

                first, second, both = slice(0, P), slice(P, N), slice(0, N)
                if step == 6:
                    pe.wait_ge(q_ok, b + 1)
                    pe.wait_ge(k_ok, b + 1)
                    if b > 0:
                        pe.wait_ge(p2_ok, b)
                    else:
                        pe.wait_ge(bn_ok, 1)
                        pe.wait_ge(w2s_ok, 1)
                        pe.wait_ge(cm_ok, 1)
                        pe.wait_ge(v_const, 6)
                    mixed = A[:, 0, :].rearrange("p (g t j) -> p t g j", g=2, t=2)

                    def second_queries(t):
                        bank = A[:, 1 + t, :].rearrange("p (g j) -> p g j", g=2)
                        for g in range(2):
                            mm(bank[:, g, :], rows(q_s, 2 * g + t, second), rows(k_s, 2 * g + t, both),
                               start=(g == 0), stop=False)
                        mm(bank[:, :, second], ident_bf[:, :], causal_bf[:, :].unsqueeze(1).to_broadcast([P, 2, P]),
                           start=False).then_inc(s2b_ps, 1)

                    masked_pair(mixed[:, 0, :, :], 0, q_s, k_s, first, ident_bf, causal_bf, True, False)\
                        .then_inc(rows_done, 1)
                    second_queries(0)
                    pe.wait_ge(rows_done, 2 * b + 1)
                    masked_pair(mixed[:, 1, :, :], 1, q_s, k_s, first, ident_bf, causal_bf, False, True)\
                        .then_inc(s2a_ps, 1)
                    second_queries(1)
                if step == 7:
                    pe.wait_ge(m2_ok, NB * (b + 1))
                    mixed = A[:, 2, :].rearrange("p (g t i) -> p t g i", g=2, t=2)

                    def first_keys(t):
                        bank = A[:, t, :].rearrange("p (g i) -> p g i", g=2)
                        for g in range(2):
                            mm(bank[:, g, :], rows(k_s, 2 * g + t, first), rows(q_s, 2 * g + t, both),
                               start=(g == 0), stop=False)
                        mm(bank[:, :, first], causal_bf[:, :], ident_bf[:, :].unsqueeze(1).to_broadcast([P, 2, P]),
                           start=False, stop=False)

                    masked_pair(mixed[:, 0, :, :], 0, k_s, q_s, second, causal_bf, ident_bf, True, False)\
                        .then_inc(rows_done, 1)
                    first_keys(0)
                    first_keys(1)
                    pe.wait_ge(rows_done, 2 * b + 2)
                    masked_pair(mixed[:, 1, :, :], 1, k_s, q_s, second, causal_bf, ident_bf, False, False)
                    pe.wait_ge(d2_ok, NB * (b + 1))
                    by_head = diag2[b][:, :, :, :].rearrange("p (g t) n i -> p t g (n i)", t=2)
                    for t in range(2):
                        mm(A[:, t, :].rearrange("p (g i) -> p g i", g=2), ones_r[:, :], by_head[:, t, :, :], start=False)
                    mm(A[:, 2, :].rearrange("p (h i) -> p h i", h=HEADS), ones_r[:, :], diag2[b][:, :, 1, :],
                       start=False).then_inc(s2t_ps, 1)
                if step == 8:
                    pe.wait_ge(p2_ok, b + 1)
                    pe.wait_ge(v_ok, b + 1)
                    pe.wait_ge(v_ok, min(b + 2, B))
                    pe.wait_ge(t1_ok, min(b + 3, B))
                    if b > 0:
                        pe.wait_ge(y_ok, b)
                    for h in range(HEADS):
                        early = p2[b][:, h % 2, (h // 2) * N:(h // 2 + 1) * N]
                        late = p2[b][:, 2, h * P:(h + 1) * P]
                        mm(pv2[:, h, :], early[:, first], v2[b][:, 0, h, :])
                        mm(pv2[:, HEADS + h, :], early[:, second], v2[b][:, 0, h, :], stop=False)
                        last = mm(pv2[:, HEADS + h, :], late, v2[b][:, 1, h, :], start=False)
                    last.then_inc(pv2_ps, 1)
                if step == 9:
                    pe.wait_ge(y_ok, b + 1)
                    pe.wait_ge(m1_ok, B)
                    if b > 0:
                        pe.wait_ge(t2_ok, b)
                    for n in range(NB):
                        last = pe.transpose(Q[0][0:C, n * P:(n + 1) * P], y2[b][:, n, :], ident)
                    last.then_inc(yT_ps, 1)
                if step == 10:
                    pe.wait_ge(yT_ok, b + 1)
                    for n in range(NB):
                        last = mm(Q[0][:, N + n * C:N + (n + 1) * C], yT[b][:, n * P:(n + 1) * P], attn_proj[:, :])
                    last.then_inc(pj_ps, 1)
                if step == 11:
                    pe.wait_ge(p1_ok, B)
                    if b > 0:
                        pe.wait_ge(ln[1]["s_TT"], b)
                    transposed(1, b, Q[1])
                if step == 12 and b % SB == SB - 1:
                    s = b // SB
                    pe.wait_ge(ln[1]["s_TT"], b + 1)
                    if s == 0:
                        pe.wait_ge(w1_ok, 1)
                        pe.wait_ge(q_ok, B)
                        pe.wait_ge(k_ok, B)
                    for q in range(PAIRS):
                        n = PAIRS * s + q
                        if n >= 2:
                            pe.wait_ge(h1_ok, n - 1)
                        for part, w in enumerate((w1_hi, w1_lo)):
                            last = mm(PR[n % 2][:, :], w[:, q * P:(q + 1) * P],
                                      x2T[:, SB * s:SB * (s + 1), :].rearrange("p b n -> p (b n)"),
                                      start=(part == 0), stop=(part == 1))
                        last.then_inc(l1_ps, 1)
            pe.wait_ge(xsum_ok, B - 1)
            pe.wait_ge(wr_ok, 1)
            pe.wait_ge(y_ok, B)
            for n in range(NB):
                out = M[:, n * E:(n + 1) * E]
                mm(out, xsum[B - 2][:, n * P:(n + 1) * P], wr4[:, :], stop=False)
                last = mm(out, ones_f[0:1, :], br[:, :], start=False)
            last.then_inc(g_ps, 1)

            ring = [Q[0], Q[1], PR[0], PR[1]]

            def second_layer(s, q):
                n = PAIRS * s + q
                pe.wait_ge(h1_ok, PAIRS * s + q + 1)
                if n == 0:
                    pe.wait_ge(t2_ok, B)
                if n == 1:
                    pe.wait_ge(ln[1]["s_TT"], B)
                if n in (2, 3):
                    pe.wait_ge(h1_ok, 2 * PAIRS)
                if n >= 4:
                    pe.wait_ge(h2_ok, n - 3)
                mm(ring[n % 4][:, :], w2s[:, q, :], h1[:, q, SB * N * s:SB * N * (s + 1)]).then_inc(l2_ps, 1)

            def third_layer(s, q):
                n = PAIRS * s + q
                out = A[0:C, 2 * (1 - s), :]
                pe.wait_ge(h2_ok, n + 1)
                last = mm(out, wo[:, q, :], h2[n % 4][:, :, :].rearrange("p b n -> p (b n)"), start=(q == 0),
                          stop=False)
                last.then_inc(l3_step, 1)
                if q == PAIRS - 1:
                    for i in range(SB * NB):
                        last = mm(out[:, i * P:(i + 1) * P], t2[SB * s + i // NB][:, i % NB, :], ident,
                                  start=False, stop=(i == SB * NB - 1))
                    last.then_inc(l3_ps, 1)

            second_layer(0, 0)
            pe.wait_ge(g_ok, 1)
            for n in range(NB):
                last = pe.transpose(M[0:E, N + n * P:N + (n + 1) * P], gw[:, n, :], ident)
            last.then_inc(gT_ps, 1)
            second_layer(0, 1)
            pe.wait_ge(gT_ok, 1)
            pe.wait_ge(sel_ok, 1)
            pe.wait_ge(p2_ok, B)
            for q in range(PAIRS):
                last = mm(A[:, q // 2, (q % 2) * N:(q % 2 + 1) * N],
                          pair_sel[:, 2 * q:2 * q + 2, :].rearrange("e t c -> e (t c)"), gwT[:, :])
                if q % 2:
                    last.then_inc(wb_ps, 1)
            mm(M[0:C, 0:N], cmat[:, :], gwT[:, :]).then_inc(cw_ps, 1)
            second_layer(0, 2)
            second_layer(0, 3)
            for s in range(B // SB):
                if s == 1:
                    pe.wait_ge(wb_ok, 2)
                for q in range(PAIRS):
                    third_layer(s, q)
                    if s + 1 < B // SB:
                        second_layer(s + 1, q)


_INS = ["x", "L0_conv_Wg", "L0_conv_bg", "L0_conv_Wt", "L0_conv_bt", "L0_conv_Wp", "L0_conv_bp", "L0_conv_Wo",
        "L0_conv_bo", "L1_attn_W_attn", "L1_attn_W_proj", "L1_ffn_Wr", "L1_ffn_br", "L1_ffn_W1", "L1_ffn_b1",
        "L1_ffn_g1", "L1_ffn_be1", "L1_ffn_m1", "L1_ffn_v1", "L1_ffn_W2", "L1_ffn_b2", "L1_ffn_g2", "L1_ffn_be2",
        "L1_ffn_m2", "L1_ffn_v2", "L1_ffn_Wo", "L1_ffn_bo"]


def kernel(**inputs):
    import numpy as _np
    import concourse.bacc as _bacc
    from concourse import mybir as _mybir
    from concourse.bass_utils import run_bass_kernel_spmd as _run

    nc = _bacc.Bacc("TRN2", target_bir_lowering=False, num_devices=1)
    arrays, args = {}, {}
    for name in _INS + ["constants"]:
        v = shape_constants() if name == "constants" else _np.ascontiguousarray(inputs[name])
        arrays[f"in_{name}_dram"] = v
        args[name] = nc.dram_tensor(f"in_{name}_dram", v.shape, _mybir.dt.from_np(v.dtype), kind="ExternalInput").ap()
    args["out"] = nc.dram_tensor("out_0_dram", inputs["x"].shape, _mybir.dt.float32, kind="ExternalOutput").ap()
    conv_attention_moe(nc, args)
    r = _run(nc, [arrays], core_ids=[0])
    return r.results[0]["out_0_dram"]
```

```python
from contextlib import ExitStack

import numpy as np

import concourse.bass as bass
from concourse import mybir

F32 = mybir.dt.float32
F32R = mybir.dt.float32r
BF16 = mybir.dt.bfloat16
ALU = mybir.AluOpType
ACT = mybir.ActivationFunctionType
X = mybir.AxisListType.X

P = 128
MASKED = -3.0e38
EPS_LN = 1e-5
EPS_BN = 1e-3

SHAPES = dict(B=4, C=64, CI=32, E=8)
ROLE_THETA, ROLE_PHI, ROLE_Q, ROLE_K = range(4)
PACKS = {
    "conv": (("ident", 128), ("roles", 4), ("th4", 256), ("vx", 129), ("g", 65), ("woT", 64)),
    "attn": (("qkv", 192), ("proj", 64), ("causal", 128), ("bn", 40)),
    "ffn": (("w1", 512), ("w2", 512), ("wo", 256), ("wr", 8), ("br", 8), ("bo", 64)),
}


def columns(pack):
    at, start = {}, 0
    for name, n in PACKS[pack]:
        at[name] = slice(start, start + n)
        start += n
    return at, start


def laid_out(inputs):
    w = {n: np.asarray(inputs[n]) for n in inputs}
    C, CI, E = SHAPES["C"], SHAPES["CI"], SHAPES["E"]
    packs = {}
    for pack in PACKS:
        at, n = columns(pack)
        a = np.zeros((P, n), np.float32)
        packs[pack] = a, {name: a[:, at[name]] for name in at}
    p = np.arange(P)
    v = packs["conv"][1]
    v["ident"][:] = np.eye(P)
    for r, rows in ((ROLE_THETA, 32), (ROLE_PHI, 64), (ROLE_Q, 16), (ROLE_K, 32)):
        v["roles"][:, r] = -((p // rows) % 2)
    for i, n in enumerate("tp"):
        for r in range(4):
            c = i * P + r * CI
            v["th4"][0:C, c:c + CI] = w[f"L0_conv_W{n}"].T
            v["th4"][C, c:c + CI] = w[f"L0_conv_b{n}"]
    v["vx"][C, C] = 1.0
    v["vx"][0:C, C + 1:] = np.eye(C)
    v["vx"][C, C + 1:] = w["L0_conv_bo"]
    v["g"][0:CI, 0:C] = w["L0_conv_Wg"]
    v["g"][0:CI, C] = w["L0_conv_bg"]
    v["woT"][0:CI, :] = w["L0_conv_Wo"].T
    v = packs["attn"][1]
    for half in range(2):
        v["qkv"][half * C:half * C + C, :] = w["L1_attn_W_attn"]
    v["proj"][0:C, :] = w["L1_attn_W_proj"]
    v["causal"][:] = np.where(p[None, :] > p[:, None], MASKED, 0.0)
    for i in range(2):
        for j, n in enumerate(("g", "b", "m", "v", "be")):
            c = (5 * i + j) * 4
            v["bn"][:, c:c + 4] = w[f"L1_ffn_{n}{i + 1}"].reshape(4, P).T
    v = packs["ffn"][1]
    for half in range(2):
        v["w1"][half * C:half * C + C, :] = w["L1_ffn_W1"].transpose(1, 0, 2).reshape(C, E * C)
        v["wr"][half * C:half * C + C, :] = w["L1_ffn_Wr"]
    for e in range(E):
        rows, c = (e % 2) * C, e // 2 * P + (e % 2) * C
        v["w2"][rows:rows + C, c:c + C] = w["L1_ffn_W2"][e]
    v["wo"][:] = w["L1_ffn_Wo"].reshape(4, P, C).transpose(1, 0, 2).reshape(P, 4 * C)
    v["br"][0, :] = w["L1_ffn_br"]
    v["bo"][0:E, :] = w["L1_ffn_bo"]
    return {f"pack_{pack}": packs[pack][0] for pack in packs}


def conv_attention_moe(nc, a):
    B, C, H, W = a["x"].shape
    N = H * W
    CI, E = SHAPES["CI"], SHAPES["E"]
    NB = N // P
    HEADS, HS = 4, C // 4
    PAIRS = E * C // P
    assert (B, C, N, CI, NB, E, PAIRS) == (4, 64, 256, 32, 2, 8, 4)
    SB = 2
    VW = HS + 1
    CX = 2 * C + 1

    with ExitStack() as ctx:
        def sb(name, shape, dt=F32):
            return ctx.enter_context(nc.sbuf_tensor(name, shape, dt))

        def ps(name, shape):
            return ctx.enter_context(nc.psum_tensor(name, shape, F32))

        def sem(name):
            return ctx.enter_context(nc.semaphore(name))

        packs = {}
        for pack in PACKS:
            at, n = columns(pack)
            tile = sb(f"pack_{pack}", [P, n])
            packs[pack] = tile
            packs |= {f"{pack}.{name}": tile[:, at[name]] for name in at}
        ident = packs["conv.ident"]
        role = [packs["conv.roles"][:, i:i + 1] for i in range(4)]
        conv_th4 = packs["conv.th4"][0:C + 1, :].rearrange("c (t p) -> c t p", t=2)
        conv_vx = packs["conv.vx"][0:C + 1, :]
        conv_g, conv_woT = packs["conv.g"][0:CI, :], packs["conv.woT"][0:CI, :]
        attn_w, attn_proj = packs["attn.qkv"], packs["attn.proj"][0:C, :]
        bn = packs["attn.bn"].rearrange("p (a v q) -> p a v q", a=2, v=5)
        w1, wr = packs["ffn.w1"], packs["ffn.wr"]
        w2 = packs["ffn.w2"].rearrange("p (q k) -> p q k", q=PAIRS)
        wo = packs["ffn.wo"].rearrange("p (q c) -> p q c", q=PAIRS)
        br, bo = packs["ffn.br"][0:1, :], packs["ffn.bo"][0:E, :]
        neg_ident = sb("neg_ident", [P, P])
        ident_bf = sb("ident_bf", [P, P], BF16)
        causal_bf = sb("causal_bf", [P, P], BF16)
        ones_r = sb("ones_r", [P, P], F32R)
        ones_f = sb("ones_f", [P, P])
        attn_qk = sb("attn_qk", [P, 2, HEADS, HS])
        attn_qk_hi = sb("attn_qk_hi", [P, 2, HEADS, 4, HS], F32R)
        attn_qk_lo = sb("attn_qk_lo", [P, 2, HEADS, 4, HS], F32R)
        attn_v_hi = sb("attn_v_hi", [P, C], F32R)
        attn_v_lo = sb("attn_v_lo", [P, C], F32R)
        w1_hi = sb("w1_hi", [P, E * C], F32R)
        w1_lo = sb("w1_lo", [P, E * C], F32R)
        w2s = sb("w2s", [P, PAIRS, P])
        bn_var = sb("bn_var", [P, 2, PAIRS])
        bn_rs = sb("bn_rs", [P, 2, PAIRS])
        bn_s = sb("bn_s", [P, 2, PAIRS])
        bn_d = sb("bn_d", [P, 2, PAIRS])
        bn_ds = sb("bn_ds", [P, 2, PAIRS])
        bn_c = sb("bn_c", [P, 2, PAIRS])
        bn_nc = sb("bn_nc", [P, PAIRS])
        s2_diag = sb("s2_diag", [P, PAIRS, P])
        c2_blk = sb("c2_blk", [P, PAIRS * E])
        wr4 = sb("wr4", [P, E])
        cmat = sb("cmat", [E, C])
        pair_sel = sb("pair_sel", [E, E, C])
        half = sb("half", [P, 2 * PAIRS])

        warm = sb("warm", [P, 512], BF16)

        def per_batch(name, shape, dt=F32):
            return [sb(f"{name}{b}", shape, dt) for b in range(B)]

        def two(name, shape, dt=F32):
            return [sb(f"{name}{i}", shape, dt) for i in range(2)] * (B // 2)

        x1 = sb("x1", [C + 1, B, N])
        f_tmp = per_batch("f_tmp", [P, 2, N], F32R)
        th_s = per_batch("th_s", [P, N], F32R)
        ph_s = per_batch("ph_s", [P, N], F32R)
        vx = per_batch("vx", [P, NB, CX])
        m1 = per_batch("m1", [P, NB])
        diag1 = per_batch("diag1", [P, NB, P], F32R)
        p1 = per_batch("p1", [P, NB, N])
        r1 = per_batch("r1", [P, NB])
        t1 = per_batch("t1", [P, NB, C])
        t2 = per_batch("t2", [P, NB, C])
        ln = [dict(st=per_batch(f"ln{i}_st", [P, NB, 6]), mv=per_batch(f"ln{i}_mv", [P, NB, 2]),
                   var=per_batch(f"ln{i}_var", [P, NB]), rs=per_batch(f"ln{i}_rs", [P, NB]),
                   xh=per_batch(f"ln{i}_xh", [P, NB, C]), xs=per_batch(f"ln{i}_xs", [P, NB, 2, C]))
              for i in range(2)]
        xT = per_batch("xT", [P, N], F32R)
        x2T = sb("x2T", [P, B, N], F32R)
        qk_tmp = two("qk_tmp", [P, 2, 2 * N], F32R)
        q_s = per_batch("q_s", [P, 2, N], F32R)
        k_s = per_batch("k_s", [P, 2, N], F32R)
        v2 = per_batch("v2", [P, NB, HEADS, VW])
        m2 = per_batch("m2", [P, NB, HEADS])
        diag2 = two("diag2", [P, HEADS, NB, P], F32R)
        p2 = two("p2", [P, 3, 512])
        r2 = per_batch("r2", [P, NB * HEADS])
        y2 = per_batch("y2", [P, NB, C])
        yT = per_batch("yT", [C, N])
        h1 = sb("h1", [P, PAIRS, B * N])
        xsum = [sb(f"xsum{i}", [P, N]) for i in range(B - 1)]
        gm = sb("gm", [P, NB])
        gl = sb("gl", [P, NB, E])
        ge = sb("ge", [P, NB, E])
        gs = sb("gs", [P, NB])
        gr = sb("gr", [P, NB])
        gw = sb("gw", [P, NB, E])
        gwT = sb("gwT", [E, N])
        w_b = sb("w_b", [P, PAIRS, N])
        cw = sb("cw", [C, N])
        h2 = [sb(f"h2_{i}", [P, SB, N]) for i in range(4)]
        o_sb = [sb(f"o_sb{i}", [C, SB, N]) for i in range(B // SB)]

        A = ps("A", [P, 3, 512])
        PR = [ps(f"PR{i}", [P, 512]) for i in range(2)]
        Q = [ps(f"Q{i}", [P, 512]) for i in range(2)]
        M = ps("M", [P, 512])
        pv1 = M[:, 0:NB * (C + 1)].rearrange("p (n c) -> p n c", n=NB)
        vps = M[:, 130:130 + NB * C]
        pv2 = M[:, 258:258 + NB * HEADS * VW].rearrange("p (n c) -> p n c", c=VW)

        x_in = [sem(f"x_in{i}") for i in range(2)]
        conv_in, attn_in, ffn_in, out_done = map(sem, ("conv_in", "attn_in", "ffn_in", "out_done"))
        x_ones = sem("x_ones")
        warm_ok = sem("warm_ok")
        filled = sem("filled")
        v_const = sem("v_const")
        vx_w, vxw_ok = sem("vx_w"), sem("vxw_ok")
        aw_scaled, aw_hi, aw_ok = map(sem, ("aw_scaled", "aw_hi", "aw_ok"))
        w1_rounded, w1_ok = sem("w1_rounded"), sem("w1_ok")
        bn_step, bn_pow, s2d_ok, s2_b, w2s_ok = map(
            sem, ("bn_step", "bn_pow", "s2d_ok", "s2_b", "w2s_ok"))
        c2_ok, cm_ps, cm_ok, wr_ok, sel_ok = map(sem, ("c2_ok", "cm_ps", "cm_ok", "wr_ok", "sel_ok"))
        f_ps, vx_ps, f_rnd, f_split, vx_ok = map(sem, ("f_ps", "vx_ps", "f_rnd", "f_split", "vx_ok"))
        s1_ps, m1_ok, d1_ok, s1t_ps, p1_ok, pv1_ps, r1_ok, t1_ok = map(
            sem, ("s1_ps", "m1_ok", "d1_ok", "s1t_ps", "p1_ok", "pv1_ps", "r1_ok", "t1_ok"))
        for i, l in enumerate(ln):
            for n in ("stats", "aggr", "eps", "pow", "xh", "hi", "xs", "T", "TT"):
                l["s_" + n] = sem(f"ln{i}_s_{n}")
        q_ps, k_ps, v_ps, q_rnd, k_rnd, q_ok, k_ok, v_ok = map(
            sem, ("q_ps", "k_ps", "v_ps", "q_rnd", "k_rnd", "q_ok", "k_ok", "v_ok"))
        s2a_ps, s2b_ps, m2_ok, d2_ok, s2t_ps, p2_ok = map(
            sem, ("s2a_ps", "s2b_ps", "m2_ok", "d2_ok", "s2t_ps", "p2_ok"))
        pv2_ps, r2_ok, y_ok, yT_ps, yT_ok, pj_ps, t2_ok = map(
            sem, ("pv2_ps", "r2_ok", "y_ok", "yT_ps", "yT_ok", "pj_ps", "t2_ok"))
        rows_done = sem("rows_done")
        l1_ps, h1_ok, xsum_ok = map(sem, ("l1_ps", "h1_ok", "xsum_ok"))
        g_ps, g_step, g_exp, g_ok, gT_ps, gT_ok, wb_ps, wb_ok, cw_ps, cw_ok = map(
            sem, ("g_ps", "g_step", "g_exp", "g_ok", "gT_ps", "gT_ok", "wb_ps", "wb_ok", "cw_ps", "cw_ok"))
        l2_ps, h2_ok, l3_step, l3_ps, o_ok = map(sem, ("l2_ps", "h2_ok", "l3_step", "l3_ps", "o_ok"))

        STEPS, LAG = 13, 2
        WARM_UP = 14

        def schedule():
            for s in range(STEPS + LAG * (B - 1)):
                for b in range(B):
                    if 0 <= s - LAG * b < STEPS:
                        yield s - LAG * b, b

        block = ctx.enter_context(nc.Block())

        @block.sync
        def _(sp):
            xv = a["x"].rearrange("b c h w -> b c (h w)").rearrange("b c n -> c b n")
            sp.dma_start(x1[0:C, 0, :], xv[:, 0, :]).then_inc(x_in[0], 16)
            sp.dma_start(x1[0:C, 1:B, :], xv[:, 1:B, :]).then_inc(x_in[1], 16)
            sp.dma_start(packs["attn"][:, :], a["pack_attn"]).then_inc(attn_in, 16)
            sp.dma_start(packs["ffn"][:, :], a["pack_ffn"]).then_inc(ffn_in, 16)
            ov = a["out"].rearrange("b c h w -> b c (h w)").rearrange("b c n -> c b n")
            for s in range(B // SB):
                sp.wait_ge(o_ok, s + 1)
                sp.dma_start(ov[:, SB * s:SB * s + SB, :], o_sb[s][:, :, :]).then_inc(out_done, 16)
            sp.wait_ge(out_done, 16 * (B // SB))

        @block.gpsimd
        def _(pool):
            pool.memset(ones_f[:, :], 1.0).then_inc(filled, 1)
            pool.memset(half[:, :], -0.5).then_inc(filled, 1)
            pool.memset(c2_blk[:, :], 0.0).then_inc(filled, 1)
            for b in range(B):
                pool.memset(v2[b][:, :, :, :], 1.0).then_inc(filled, 1)

            def diagonal(out, m, batch_dims):
                n = m.shape[1]
                return pool.tensor_tensor(out, neg_ident[:, :].unsqueeze(1).to_broadcast([P, n, P]),
                                          m.unsqueeze(2).to_broadcast([P, n, P]), ALU.mult)

            def root(i, b):
                pool.wait_ge(ln[i]["s_eps"], b + 1)
                pool.tensor_tensor(ln[i]["rs"][b][:, :], ln[i]["var"][b][:, :], half[:, 0:NB],
                                   ALU.pow).then_inc(ln[i]["s_pow"], 1)

            for step, b in schedule():
                if step == 1:
                    if b == 0:
                        pool.wait_ge(v_const, 2)
                        pool.wait_ge(filled, 2)
                    pool.wait_ge(m1_ok, b + 1)
                    diagonal(diag1[b][:, :, :], m1[b][:, :], 1).then_inc(d1_ok, 1)
                if step == 3:
                    root(0, b)
                    if b == 0:
                        pool.wait_ge(bn_step, 1)
                        pool.tensor_tensor(bn_rs[:, :, :].rearrange("p a q -> p (a q)"),
                                           bn_var[:, :, :].rearrange("p a q -> p (a q)"), half[:, :],
                                           ALU.pow).then_inc(bn_pow, 1)
                        pool.wait_ge(bn_step, 3)
                        pool.tensor_tensor(s2_diag[:, :, :], ident.unsqueeze(1).to_broadcast([P, PAIRS, P]),
                                           bn_s[:, 1, :].unsqueeze(2).to_broadcast([P, PAIRS, P]),
                                           ALU.mult).then_inc(s2d_ok, 1)
                if step == 6:
                    if b > 1:
                        pool.wait_ge(s2t_ps, b - 1)
                    for i in range(NB):
                        pool.wait_ge(m2_ok, NB * b + i + 1)
                        diagonal(diag2[b][:, :, i, :], m2[b][:, i, :], 1).then_inc(d2_ok, 1)
                if step == 10:
                    root(1, b)
                if step == 11 and b > 0:
                    pool.wait_ge(ln[1]["s_TT"], b + 1)
                    if b > 1:
                        pool.wait_ge(xsum_ok, b - 1)
                    first = (x2T[:, 0, :].bitcast(F32) if b == 1 else xsum[b - 2][:, :])
                    pool.tensor_tensor(xsum[b - 1][:, :], first, x2T[:, b, :].bitcast(F32),
                                       ALU.add).then_inc(xsum_ok, 1)

        @block.scalar
        def _(act):
            act.dma_start(packs["conv"][:, :], a["pack_conv"]).then_inc(conv_in, 16)

            def copy(out, in_):
                return act.activation(out, in_, ACT.Copy)

            act.wait_ge(vx_w, 1)
            copy(conv_vx[:, 0:C], Q[1][0:C + 1, 0:C]).then_inc(vxw_ok, 1)

            def xT_copy(i, b, out, bank):
                act.wait_ge(ln[i]["s_T"], b + 1)
                copy(out, bank[:, 0:N]).then_inc(ln[i]["s_TT"], 1)

            for step, b in schedule():
                if step == 0:
                    act.wait_ge(f_ps, b + 1)
                    copy(f_tmp[b][:, :, :], Q[b % 2][:, :].rearrange("p (t n) -> p t n", t=2)).then_inc(f_rnd, 1)
                    act.wait_ge(vx_ps, b + 1)
                    copy(vx[b][:, :, :], PR[0][:, 0:NB * CX].rearrange("p (n c) -> p n c", n=NB)).then_inc(vx_ok, 1)
                if step == 2:
                    act.wait_ge(s1t_ps, b + 1)
                    act.activation(p1[b][:, :, :], Q[b % 2][:, :].rearrange("p (n i) -> p n i", n=NB),
                                   ACT.Exp).then_inc(p1_ok, 1)
                if step == 4:
                    xT_copy(0, b, xT[b][:, :], PR[1])
                    if b == 0:
                        act.wait_ge(cm_ps, 1)
                        copy(cmat[:, :], A[0:E, 2, 0:C]).then_inc(cm_ok, 1)
                if step == 5:
                    act.wait_ge(v_ps, b + 1)
                    act.wait_ge(filled, 4 + b)
                    copy(v2[b][:, :, :, 0:HS], vps.rearrange("p (n h d) -> p n h d", n=NB, h=HEADS)).then_inc(v_ok, 1)
                    if b > 1:
                        act.wait_ge(k_ok, b - 1)
                    act.wait_ge(q_ps, b + 1)
                    copy(qk_tmp[b][:, 0, :], PR[0][:, :]).then_inc(q_rnd, 1)
                    act.wait_ge(k_ps, b + 1)
                    copy(qk_tmp[b][:, 1, :], PR[1][:, :]).then_inc(k_rnd, 1)
                if step == 7:
                    act.wait_ge(s2t_ps, b + 1)
                    if b > 1:
                        act.wait_ge(pv2_ps, b - 1)
                    act.activation(p2[b][:, :, :], A[:, :, :], ACT.Exp).then_inc(p2_ok, 1)
                if step == 9:
                    act.wait_ge(yT_ps, b + 1)
                    copy(yT[b][:, :], Q[0][0:C, 0:N]).then_inc(yT_ok, 1)
                if step == 11:
                    xT_copy(1, b, x2T[:, b, :], Q[1])
                if step == 12 and b % SB == SB - 1:
                    s = b // SB
                    if s == 0:
                        act.wait_ge(bn_step, 6)
                    for q in range(PAIRS):
                        n = PAIRS * s + q
                        act.wait_ge(l1_ps, n + 1)
                        act.activation(h1[:, q, SB * N * s:SB * N * (s + 1)], PR[n % 2][:, :], ACT.Relu,
                                       bias=bn_c[:, 0, q:q + 1], scale=bn_s[:, 0, q:q + 1]).then_inc(h1_ok, 1)
            act.wait_ge(g_step, 2)
            act.activation(ge[:, :, :], gl[:, :, :], ACT.Exp).then_inc(g_exp, 1)
            act.wait_ge(gT_ps, 1)
            copy(gwT[:, :], M[0:E, N:2 * N]).then_inc(gT_ok, 1)
            for i in range(2):
                act.wait_ge(wb_ps, i + 1)
                copy(w_b[:, 2 * i:2 * i + 2, :], A[:, i, :].rearrange("p (q n) -> p q n", q=2)).then_inc(wb_ok, 1)
            act.wait_ge(cw_ps, 1)
            copy(cw[:, :], M[0:C, 0:N]).then_inc(cw_ok, 1)

        @block.vector
        def _(v):
            def mul_add(out, in0, scalar, in1):
                return v.scalar_tensor_tensor(out=out, in0=in0, scalar=scalar, in1=in1, op0=ALU.mult, op1=ALU.add)

            v.memset(warm[:, :], 0.0).then_inc(warm_ok, 1)
            v.memset(x1[C:C + 1, :, :], 1.0).then_inc(x_ones, 1)
            v.memset(ones_r[:, :].bitcast(F32), 1.0).then_inc(v_const, 1)
            v.wait_ge(conv_in, 16)
            v.tensor_scalar(neg_ident[:, :], ident, -1.0, None, ALU.mult).then_inc(v_const, 1)
            v.tensor_copy(ident_bf[:, :], ident).then_inc(v_const, 1)

            def attention_weights():
                v.wait_ge(attn_in, 16)
                v.tensor_copy(causal_bf[:, :], packs["attn.causal"]).then_inc(v_const, 1)
                v.tensor_scalar(attn_qk[:, 0, :, :], attn_w[:, 0:C].rearrange("p (h d) -> p h d", h=HEADS),
                                float(HS) ** -0.5, None, ALU.mult).then_inc(aw_scaled, 1)
                v.tensor_copy(attn_qk[:, 1, :, :], attn_w[:, C:2 * C].rearrange("p (h d) -> p h d", h=HEADS))\
                    .then_inc(aw_scaled, 1)
                v.tensor_copy(attn_v_hi[:, :], attn_w[:, 2 * C:3 * C]).then_inc(aw_hi, 1)
                v.wait_ge(aw_scaled, 2)
                four = [attn_qk[:, i, :, :].unsqueeze(2).to_broadcast([P, HEADS, 4, HS]) for i in range(2)]
                for i in range(2):
                    v.tensor_copy(attn_qk_hi[:, i, :, :, :], four[i]).then_inc(aw_hi, 1)
                v.wait_ge(aw_hi, 3)
                for i in range(2):
                    v.tensor_tensor(attn_qk_lo[:, i, :, :, :], four[i], attn_qk_hi[:, i, :, :, :].bitcast(F32),
                                    ALU.subtract).then_inc(aw_ok, 1)
                v.tensor_tensor(attn_v_lo[:, :], attn_w[:, 2 * C:3 * C], attn_v_hi[:, :].bitcast(F32),
                                ALU.subtract).then_inc(aw_ok, 1)

            def norm_parameters(part):
                g, bb, m, var, be = (bn[:, :, j, :] for j in range(5))
                if part == 0:
                    v.wait_ge(attn_in, 16)
                    v.tensor_scalar(bn_var[:, :, :], var, EPS_BN, None, ALU.add).then_inc(bn_step, 1)
                    v.tensor_tensor(bn_d[:, :, :], bb, m, ALU.subtract).then_inc(bn_step, 1)
                    return
                v.wait_ge(bn_pow, 1)
                v.tensor_tensor(bn_s[:, :, :], g, bn_rs[:, :, :], ALU.mult).then_inc(bn_step, 1)
                v.wait_ge(bn_step, 3)
                v.tensor_tensor(bn_ds[:, :, :], bn_d[:, :, :], bn_s[:, :, :], ALU.mult).then_inc(bn_step, 1)
                v.wait_ge(bn_step, 4)
                v.tensor_tensor(bn_c[:, :, :], bn_ds[:, :, :], be, ALU.add).then_inc(bn_step, 1)
                v.wait_ge(bn_step, 5)
                v.tensor_scalar(bn_nc[:, :], bn_c[:, 1, :], -1.0, None, ALU.mult).then_inc(bn_step, 1)
                v.wait_ge(filled, 3)
                for t in range(2):
                    v.tensor_copy(c2_blk[C * t:C * t + C, t:t + (E + 2) * (PAIRS - 1) + 1:E + 2],
                                  bn_c[C * t:C * t + C, 1, :]).then_inc(c2_ok, 1)

            def expert_weights():
                v.wait_ge(ffn_in, 16)
                v.tensor_copy(pair_sel[:, :, :], ident[0:E, 0:E].unsqueeze(2).to_broadcast([E, E, C]))\
                    .then_inc(sel_ok, 1)
                v.tensor_copy(w1_hi[:, :], w1).then_inc(w1_rounded, 1)
                v.tensor_scalar(wr4[:, :], wr, 1.0 / B, None, ALU.mult).then_inc(wr_ok, 1)
                v.wait_ge(w1_rounded, 1)
                v.tensor_tensor(w1_lo[:, :], w1, w1_hi[:, :].bitcast(F32), ALU.subtract).then_inc(w1_ok, 1)

            def layer_norm(i, b, t, ready):
                l = ln[i]
                v.wait_ge(ready, b + 1)
                for n in range(NB):
                    v.bn_stats(l["st"][b][:, n, :], t[:, n, :]).then_inc(l["s_stats"], 1)
                for n in range(NB):
                    v.wait_ge(l["s_stats"], NB * b + n + 1)
                    v.bn_aggr(l["mv"][b][:, n, :], l["st"][b][:, n, :]).then_inc(l["s_aggr"], 1)
                v.wait_ge(l["s_aggr"], NB * (b + 1))
                v.tensor_scalar(l["var"][b][:, :], l["mv"][b][:, :, 1], EPS_LN, None, ALU.add).then_inc(l["s_eps"], 1)

            def normed(i, b, t):
                l = ln[i]
                v.wait_ge(l["s_pow"], b + 1)
                for n in range(NB):
                    v.tensor_scalar(l["xh"][b][:, n, :], t[:, n, :], l["mv"][b][:, n, 0:1], l["rs"][b][:, n:n + 1],
                                    ALU.subtract, ALU.mult).then_inc(l["s_xh"], 1)
                v.wait_ge(l["s_xh"], NB * (b + 1))
                v.tensor_copy(l["xs"][b][:, :, 0, :].bitcast(F32R), l["xh"][b][:, :, :]).then_inc(l["s_hi"], 1)
                v.wait_ge(l["s_hi"], b + 1)
                v.tensor_tensor(l["xs"][b][:, :, 1, :], l["xh"][b][:, :, :], l["xs"][b][:, :, 0, :],
                                ALU.subtract).then_inc(l["s_xs"], 1)

            for step, b in schedule():
                if step == 0:
                    v.wait_ge(f_rnd, b + 1)
                    for i, (out, r) in enumerate(((th_s, ROLE_THETA), (ph_s, ROLE_PHI))):
                        mul_add(out[b][:, :], f_tmp[b][:, i, :].bitcast(F32), role[r],
                                Q[b % 2][:, i * N:(i + 1) * N]).then_inc(f_split, 1)
                if step == 1:
                    v.wait_ge(s1_ps, b + 1)
                    v.tensor_reduce(m1[b][:, :], Q[(b + 1) % 2][:, :].rearrange("p (n j) -> p n j", n=NB), X,
                                    ALU.max).then_inc(m1_ok, 1)
                if step == 2 and b == 0:
                    attention_weights()
                    norm_parameters(0)
                if step == 3:
                    v.wait_ge(pv1_ps, b + 1)
                    v.reciprocal(r1[b][:, :], pv1[:, :, C]).then_inc(r1_ok, 1)
                    v.wait_ge(r1_ok, b + 1)
                    v.wait_ge(vx_ok, b + 1)
                    for n in range(NB):
                        i = mul_add(t1[b][:, n, :], pv1[:, n, 0:C], r1[b][:, n:n + 1], vx[b][:, n, C + 1:CX])
                    i.then_inc(t1_ok, 1)
                    layer_norm(0, b, t1[b], t1_ok)
                    if b == 0:
                        norm_parameters(1)
                    normed(0, b, t1[b])
                if step == 4 and b == 0:
                    expert_weights()
                    v.wait_ge(s2_b, 1)
                    v.tensor_tensor(w2s[:, :, :], w2, A[:, 1, :].rearrange("p (q k) -> p q k", q=PAIRS),
                                    ALU.mult).then_inc(w2s_ok, 1)
                if step == 5:
                    for i, (out, r, rnd, ok) in enumerate(((q_s, ROLE_Q, q_rnd, q_ok), (k_s, ROLE_K, k_rnd, k_ok))):
                        v.wait_ge(rnd, b + 1)
                        mul_add(out[b][:, :, :].rearrange("p g n -> p (g n)"), qk_tmp[b][:, i, :].bitcast(F32),
                                role[r], PR[i][:, :]).then_inc(ok, 1)
                if step == 6:
                    v.wait_ge(s2a_ps, b + 1)
                    v.tensor_reduce(m2[b][:, 0, :], A[:, 0, :].rearrange("p (h j) -> p h j", h=HEADS), X,
                                    ALU.max).then_inc(m2_ok, 1)
                    v.wait_ge(s2b_ps, 2 * (b + 1))
                    v.tensor_reduce(m2[b][:, 1, :].rearrange("p (g t) -> p t g", t=2),
                                    A[:, 1:3, :].rearrange("p t (g j) -> p t g j", g=2), X,
                                    ALU.max).then_inc(m2_ok, 1)
                if step == 8:
                    v.wait_ge(pv2_ps, b + 1)
                    v.reciprocal(r2[b][:, :], pv2[:, :, HS]).then_inc(r2_ok, 1)
                    v.wait_ge(r2_ok, b + 1)
                    v.tensor_tensor(y2[b][:, :, :].rearrange("p n (h d) -> p (n h) d", h=HEADS), pv2[:, :, 0:HS],
                                    r2[b][:, :].unsqueeze(2).to_broadcast([P, NB * HEADS, HS]),
                                    ALU.mult).then_inc(y_ok, 1)
                if step == 10:
                    v.wait_ge(pj_ps, b + 1)
                    v.tensor_tensor(t2[b][:, :, :], Q[0][:, N:N + NB * C].rearrange("p (n c) -> p n c", n=NB),
                                    t1[b][:, :, :], ALU.add).then_inc(t2_ok, 1)
                    layer_norm(1, b, t2[b], t2_ok)
                    normed(1, b, t2[b])
            v.wait_ge(g_ps, 1)
            logits = M[:, 0:NB * E].rearrange("p (n e) -> p n e", n=NB)
            v.tensor_reduce(gm[:, :], logits, X, ALU.max).then_inc(g_step, 1)
            v.wait_ge(g_step, 1)
            v.tensor_tensor(gl[:, :, :], logits, gm[:, :].unsqueeze(2).to_broadcast([P, NB, E]),
                            ALU.subtract).then_inc(g_step, 1)
            v.wait_ge(g_exp, 1)
            v.tensor_reduce(gs[:, :], ge[:, :, :], X, ALU.add).then_inc(g_step, 1)
            v.wait_ge(g_step, 3)
            v.reciprocal(gr[:, :], gs[:, :]).then_inc(g_step, 1)
            v.wait_ge(g_step, 4)
            v.tensor_tensor(gw[:, :, :], ge[:, :, :], gr[:, :].unsqueeze(2).to_broadcast([P, NB, E]),
                            ALU.mult).then_inc(g_ok, 1)
            ring = [Q[0], Q[1], PR[0], PR[1]]
            for s in range(B // SB):
                for q in range(PAIRS):
                    n = PAIRS * s + q
                    v.wait_ge(l2_ps, n + 1)
                    v.wait_ge(wb_ok, q // 2 + 1)
                    if n >= len(h2):
                        v.wait_ge(l3_step, n - len(h2) + 1)
                    v.scalar_tensor_tensor(out=h2[n % 4][:, :, :], in0=ring[n % 4][:, :].rearrange("p (b n) -> p b n", b=SB),
                                           scalar=bn_nc[:, q:q + 1],
                                           in1=w_b[:, q, :].unsqueeze(1).to_broadcast([P, SB, N]),
                                           op0=ALU.max, op1=ALU.mult).then_inc(h2_ok, 1)
                v.wait_ge(l3_ps, s + 1)
                v.wait_ge(cw_ok, 1)
                v.tensor_tensor(o_sb[s][:, :, :], A[0:C, 2 * (1 - s), :].rearrange("p (b n) -> p b n", b=SB),
                                cw[:, :].unsqueeze(1).to_broadcast([C, SB, N]), ALU.add).then_inc(o_ok, 1)

        @block.tensor
        def _(pe):
            def mm(out, lhsT, rhs, start=True, stop=True, **k):
                return pe.matmul(out, lhsT, rhs, start=start, stop=stop, **k)

            pe.wait_ge(warm_ok, 1)
            for _ in range(WARM_UP):
                mm(M[:, :], warm[:, 0:P], warm[:, :])

            pe.wait_ge(conv_in, 16)
            mm(Q[1][0:C + 1, 0:C], conv_g, conv_woT).then_inc(vx_w, 1)

            def transposed(i, b, bank):
                pe.wait_ge(ln[i]["s_xs"], b + 1)
                for n in range(NB):
                    last = pe.transpose(bank[:, n * P:(n + 1) * P],
                                        ln[i]["xs"][b][:, n, :, :].rearrange("p t c -> p (t c)"), ident)
                last.then_inc(ln[i]["s_T"], 1)

            for step, b in schedule():
                if step == 0:
                    pe.wait_ge(x_in[min(b, 1)], 16)
                    if b == 0:
                        pe.wait_ge(x_ones, 1)
                    else:
                        pe.wait_ge(m1_ok, b)
                        pe.wait_ge(vx_ok, b)
                    for i in range(2):
                        last = mm(Q[b % 2][:, i * N:(i + 1) * N], conv_th4[:, i, :], x1[:, b, :])
                    last.then_inc(f_ps, 1)
                    if b == 0:
                        pe.wait_ge(vxw_ok, 1)
                    if b >= 3:
                        pe.wait_ge(q_ok, b - 2)
                    for n in range(NB):
                        last = mm(PR[0][:, n * CX:(n + 1) * CX], x1[:, b, n * P:(n + 1) * P], conv_vx)
                    last.then_inc(vx_ps, 1)
                if step == 1:
                    pe.wait_ge(f_split, 2 * (b + 1))
                    if b > 0:
                        pe.wait_ge(p1_ok, b)
                    for n in range(NB):
                        last = mm(Q[(b + 1) % 2][:, n * N:(n + 1) * N], th_s[b][:, n * P:(n + 1) * P], ph_s[b][:, :])
                    last.then_inc(s1_ps, 1)
                if step == 2:
                    for n in range(NB):
                        out = Q[b % 2][:, n * N:(n + 1) * N]
                        mm(out, ph_s[b][:, n * P:(n + 1) * P], th_s[b][:, :], stop=False)
                        if n == 0:
                            pe.wait_ge(d1_ok, b + 1)
                        last = mm(out, ones_r[:, :], diag1[b][:, :, :].rearrange("p n i -> p (n i)"), start=False)
                    last.then_inc(s1t_ps, 1)
                if step == 3:
                    pe.wait_ge(p1_ok, b + 1)
                    pe.wait_ge(vx_ok, b + 1)
                    if b > 0:
                        pe.wait_ge(v_ok, b)
                    if b > 2:
                        pe.wait_ge(y_ok, b - 2)
                    for i in range(NB):
                        for j in range(NB):
                            last = mm(pv1[:, i, :], p1[b][:, j, i * P:(i + 1) * P], vx[b][:, j, 0:C + 1],
                                      start=(j == 0), stop=(j == NB - 1))
                    last.then_inc(pv1_ps, 1)
                if step == 4:
                    if b > 0:
                        pe.wait_ge(k_ok, b)
                    if b == 0:
                        pe.wait_ge(s2d_ok, 1)
                        pe.wait_ge(filled, 1)
                        mm(A[:, 1, :], ones_f[:, :], s2_diag[:, :, :].rearrange("p q k -> p (q k)")).then_inc(s2_b, 1)
                        pe.wait_ge(c2_ok, 2)
                        pe.wait_ge(ffn_in, 16)
                        for q in range(PAIRS):
                            mm(A[0:E, 2, 0:C], c2_blk[:, q * E:(q + 1) * E], wo[:, q, :], start=(q == 0), stop=False)
                        mm(A[0:E, 2, 0:C], ident[0:E, 0:E], bo, start=False).then_inc(cm_ps, 1)
                    transposed(0, b, PR[1])
                if step == 5:
                    pe.wait_ge(ln[0]["s_TT"], b + 1)
                    if b == 0:
                        pe.wait_ge(aw_ok, 3)
                    pe.wait_ge(t1_ok, b + 1)
                    if b > 1:
                        pe.wait_ge(y_ok, b - 1)
                    for n in range(NB):
                        for part, w in enumerate((attn_v_hi, attn_v_lo)):
                            last = mm(vps[:, n * C:(n + 1) * C], xT[b][:, n * P:(n + 1) * P], w[:, :],
                                      start=(part == 0), stop=(part == 1))
                    last.then_inc(v_ps, 1)
                    pe.wait_ge(vx_ok, min(b + 3, B))
                    for i, (bank, ps_sem) in enumerate(((PR[0], q_ps), (PR[1], k_ps))):
                        for g in range(2):
                            for part, w in enumerate((attn_qk_hi, attn_qk_lo)):
                                last = mm(bank[:, g * N:(g + 1) * N],
                                          w[:, i, 2 * g:2 * g + 2, :, :].rearrange("p h r d -> p (h r d)"),
                                          xT[b][:, :], start=(part == 0), stop=(part == 1))
                        last.then_inc(ps_sem, 1)

                def rows(s, h, cols):
                    return s[b][64 * (h % 2):64 * (h % 2) + 64, h // 2, cols]

                def masked_pair(out, t, left, right, cols, mask_l, mask_r, start, stop):
                    for g in range(2):
                        mm(out[:, g, :], rows(left, 2 * g + t, cols), rows(right, 2 * g + t, cols),
                           start=(start and g == 0), stop=False)
                    l, r = mask_l[:, :], mask_r[:, :].unsqueeze(1).to_broadcast([P, 2, P])
                    return mm(out, l, r, start=False, stop=stop)

                first, second, both = slice(0, P), slice(P, N), slice(0, N)
                if step == 6:
                    pe.wait_ge(q_ok, b + 1)
                    pe.wait_ge(k_ok, b + 1)
                    if b > 0:
                        pe.wait_ge(p2_ok, b)
                    else:
                        pe.wait_ge(w2s_ok, 1)
                        pe.wait_ge(cm_ok, 1)
                        pe.wait_ge(v_const, 4)
                    mixed = A[:, 0, :].rearrange("p (g t j) -> p t g j", g=2, t=2)

                    def second_queries(t):
                        bank = A[:, 1 + t, :].rearrange("p (g j) -> p g j", g=2)
                        for g in range(2):
                            mm(bank[:, g, :], rows(q_s, 2 * g + t, second), rows(k_s, 2 * g + t, both),
                               start=(g == 0), stop=False)
                        mm(bank[:, :, second], ident_bf[:, :], causal_bf[:, :].unsqueeze(1).to_broadcast([P, 2, P]),
                           start=False).then_inc(s2b_ps, 1)

                    masked_pair(mixed[:, 0, :, :], 0, q_s, k_s, first, ident_bf, causal_bf, True, False)\
                        .then_inc(rows_done, 1)
                    second_queries(0)
                    pe.wait_ge(rows_done, 2 * b + 1)
                    masked_pair(mixed[:, 1, :, :], 1, q_s, k_s, first, ident_bf, causal_bf, False, True)\
                        .then_inc(s2a_ps, 1)
                    second_queries(1)
                if step == 7:
                    pe.wait_ge(m2_ok, NB * (b + 1))
                    mixed = A[:, 2, :].rearrange("p (g t i) -> p t g i", g=2, t=2)

                    def first_keys(t):
                        bank = A[:, t, :].rearrange("p (g i) -> p g i", g=2)
                        for g in range(2):
                            mm(bank[:, g, :], rows(k_s, 2 * g + t, first), rows(q_s, 2 * g + t, both),
                               start=(g == 0), stop=False)
                        mm(bank[:, :, first], causal_bf[:, :], ident_bf[:, :].unsqueeze(1).to_broadcast([P, 2, P]),
                           start=False, stop=False)

                    masked_pair(mixed[:, 0, :, :], 0, k_s, q_s, second, causal_bf, ident_bf, True, False)\
                        .then_inc(rows_done, 1)
                    first_keys(0)
                    first_keys(1)
                    pe.wait_ge(rows_done, 2 * b + 2)
                    masked_pair(mixed[:, 1, :, :], 1, k_s, q_s, second, causal_bf, ident_bf, False, False)
                    pe.wait_ge(d2_ok, NB * (b + 1))
                    by_head = diag2[b][:, :, :, :].rearrange("p (g t) n i -> p t g (n i)", t=2)
                    for t in range(2):
                        mm(A[:, t, :].rearrange("p (g i) -> p g i", g=2), ones_r[:, :], by_head[:, t, :, :], start=False)
                    mm(A[:, 2, :].rearrange("p (h i) -> p h i", h=HEADS), ones_r[:, :], diag2[b][:, :, 1, :],
                       start=False).then_inc(s2t_ps, 1)
                if step == 8:
                    pe.wait_ge(p2_ok, b + 1)
                    pe.wait_ge(v_ok, b + 1)
                    pe.wait_ge(v_ok, min(b + 2, B))
                    pe.wait_ge(t1_ok, min(b + 3, B))
                    if b > 0:
                        pe.wait_ge(y_ok, b)
                    for h in range(HEADS):
                        early = p2[b][:, h % 2, (h // 2) * N:(h // 2 + 1) * N]
                        late = p2[b][:, 2, h * P:(h + 1) * P]
                        mm(pv2[:, h, :], early[:, first], v2[b][:, 0, h, :])
                        mm(pv2[:, HEADS + h, :], early[:, second], v2[b][:, 0, h, :], stop=False)
                        last = mm(pv2[:, HEADS + h, :], late, v2[b][:, 1, h, :], start=False)
                    last.then_inc(pv2_ps, 1)
                if step == 9:
                    pe.wait_ge(y_ok, b + 1)
                    pe.wait_ge(m1_ok, B)
                    if b > 0:
                        pe.wait_ge(t2_ok, b)
                    for n in range(NB):
                        last = pe.transpose(Q[0][0:C, n * P:(n + 1) * P], y2[b][:, n, :], ident)
                    last.then_inc(yT_ps, 1)
                if step == 10:
                    pe.wait_ge(yT_ok, b + 1)
                    for n in range(NB):
                        last = mm(Q[0][:, N + n * C:N + (n + 1) * C], yT[b][:, n * P:(n + 1) * P], attn_proj)
                    last.then_inc(pj_ps, 1)
                if step == 11:
                    pe.wait_ge(p1_ok, B)
                    if b > 0:
                        pe.wait_ge(ln[1]["s_TT"], b)
                    transposed(1, b, Q[1])
                if step == 12 and b % SB == SB - 1:
                    s = b // SB
                    pe.wait_ge(ln[1]["s_TT"], b + 1)
                    if s == 0:
                        pe.wait_ge(w1_ok, 1)
                        pe.wait_ge(q_ok, B)
                        pe.wait_ge(k_ok, B)
                    for q in range(PAIRS):
                        n = PAIRS * s + q
                        if n >= 2:
                            pe.wait_ge(h1_ok, n - 1)
                        for part, w in enumerate((w1_hi, w1_lo)):
                            last = mm(PR[n % 2][:, :], w[:, q * P:(q + 1) * P],
                                      x2T[:, SB * s:SB * (s + 1), :].rearrange("p b n -> p (b n)"),
                                      start=(part == 0), stop=(part == 1))
                        last.then_inc(l1_ps, 1)
            pe.wait_ge(xsum_ok, B - 1)
            pe.wait_ge(wr_ok, 1)
            pe.wait_ge(y_ok, B)
            for n in range(NB):
                out = M[:, n * E:(n + 1) * E]
                mm(out, xsum[B - 2][:, n * P:(n + 1) * P], wr4[:, :], stop=False)
                last = mm(out, ones_f[0:1, :], br, start=False)
            last.then_inc(g_ps, 1)

            ring = [Q[0], Q[1], PR[0], PR[1]]

            def second_layer(s, q):
                n = PAIRS * s + q
                pe.wait_ge(h1_ok, PAIRS * s + q + 1)
                if n == 0:
                    pe.wait_ge(t2_ok, B)
                if n == 1:
                    pe.wait_ge(ln[1]["s_TT"], B)
                if n in (2, 3):
                    pe.wait_ge(h1_ok, 2 * PAIRS)
                if n >= 4:
                    pe.wait_ge(h2_ok, n - 3)
                mm(ring[n % 4][:, :], w2s[:, q, :], h1[:, q, SB * N * s:SB * N * (s + 1)]).then_inc(l2_ps, 1)

            def third_layer(s, q):
                n = PAIRS * s + q
                out = A[0:C, 2 * (1 - s), :]
                pe.wait_ge(h2_ok, n + 1)
                last = mm(out, wo[:, q, :], h2[n % 4][:, :, :].rearrange("p b n -> p (b n)"), start=(q == 0),
                          stop=False)
                last.then_inc(l3_step, 1)
                if q == PAIRS - 1:
                    for i in range(SB * NB):
                        last = mm(out[:, i * P:(i + 1) * P], t2[SB * s + i // NB][:, i % NB, :], ident,
                                  start=False, stop=(i == SB * NB - 1))
                    last.then_inc(l3_ps, 1)

            second_layer(0, 0)
            pe.wait_ge(g_ok, 1)
            for n in range(NB):
                last = pe.transpose(M[0:E, N + n * P:N + (n + 1) * P], gw[:, n, :], ident)
            last.then_inc(gT_ps, 1)
            second_layer(0, 1)
            pe.wait_ge(gT_ok, 1)
            pe.wait_ge(sel_ok, 1)
            pe.wait_ge(p2_ok, B)
            for q in range(PAIRS):
                last = mm(A[:, q // 2, (q % 2) * N:(q % 2 + 1) * N],
                          pair_sel[:, 2 * q:2 * q + 2, :].rearrange("e t c -> e (t c)"), gwT[:, :])
                if q % 2:
                    last.then_inc(wb_ps, 1)
            mm(M[0:C, 0:N], cmat[:, :], gwT[:, :]).then_inc(cw_ps, 1)
            second_layer(0, 2)
            second_layer(0, 3)
            for s in range(B // SB):
                if s == 1:
                    pe.wait_ge(wb_ok, 2)
                for q in range(PAIRS):
                    third_layer(s, q)
                    if s + 1 < B // SB:
                        second_layer(s + 1, q)


def kernel(**inputs):
    import numpy as _np
    import concourse.bacc as _bacc
    from concourse import mybir as _mybir
    from concourse.bass_utils import run_bass_kernel_spmd as _run

    nc = _bacc.Bacc("TRN2", target_bir_lowering=False, num_devices=1)
    arrays, args = {}, {}
    for name, v in {"x": _np.ascontiguousarray(inputs["x"]), **laid_out(inputs)}.items():
        arrays[f"in_{name}_dram"] = v
        args[name] = nc.dram_tensor(f"in_{name}_dram", v.shape, _mybir.dt.from_np(v.dtype), kind="ExternalInput").ap()
    args["out"] = nc.dram_tensor("out_0_dram", inputs["x"].shape, _mybir.dt.float32, kind="ExternalOutput").ap()
    conv_attention_moe(nc, args)
    r = _run(nc, [arrays], core_ids=[0])
    return r.results[0]["out_0_dram"]
```

```python
from contextlib import ExitStack

import numpy as np

import concourse.bass as bass
from concourse import mybir

F32 = mybir.dt.float32
F32R = mybir.dt.float32r
BF16 = mybir.dt.bfloat16
ALU = mybir.AluOpType
ACT = mybir.ActivationFunctionType
X = mybir.AxisListType.X

P = 128
MASKED = -3.0e38
EPS_LN = 1e-5
EPS_BN = 1e-3

SHAPES = dict(B=4, C=64, CI=32, E=8)
ROWS = {"conv": SHAPES["C"] + 1}
ROLE_THETA, ROLE_PHI, ROLE_Q, ROLE_K = range(4)
PACKS = {
    "conv": (("th4", 256), ("vx", 129), ("g", 65), ("woT", 64)),
    "ident": (("ident", 128), ("roles", 4), ("experts", 8)),
    "attn": (("qkv", 192), ("proj", 64), ("causal", 128), ("bn", 40)),
    "ffn": (("w1", 512), ("w2", 512), ("wo", 256), ("wr", 8), ("br", 8), ("bo", 64)),
}


def columns(pack):
    at, start = {}, 0
    for name, n in PACKS[pack]:
        at[name] = slice(start, start + n)
        start += n
    return at, start


def laid_out(inputs):
    w = {n: np.asarray(inputs[n]) for n in inputs}
    C, CI, E = SHAPES["C"], SHAPES["CI"], SHAPES["E"]
    packs = {}
    for pack in PACKS:
        at, n = columns(pack)
        a = np.zeros((P, n), np.float32)
        packs[pack] = a[0:ROWS.get(pack, P)], {name: a[:, at[name]] for name in at}
    B, N = w["x"].shape[0], w["x"].shape[2] * w["x"].shape[3]
    x1 = np.ones((C + 1, B, N), np.float32)
    x1[0:C] = w["x"].reshape(B, C, N).transpose(1, 0, 2)
    p = np.arange(P)
    v = packs["ident"][1]
    v["ident"][:] = np.eye(P)
    for r, rows in ((ROLE_THETA, 32), (ROLE_PHI, 64), (ROLE_Q, 16), (ROLE_K, 32)):
        v["roles"][:, r] = -((p // rows) % 2)
    v["experts"][:] = p[:, None] % E == np.arange(E)
    v = packs["conv"][1]
    for i, n in enumerate("tp"):
        for r in range(4):
            c = i * P + r * CI
            v["th4"][0:C, c:c + CI] = w[f"L0_conv_W{n}"].T
            v["th4"][C, c:c + CI] = w[f"L0_conv_b{n}"]
    v["vx"][C, C] = 1.0
    v["vx"][0:C, C + 1:] = np.eye(C)
    v["vx"][C, C + 1:] = w["L0_conv_bo"]
    v["g"][0:CI, 0:C] = w["L0_conv_Wg"]
    v["g"][0:CI, C] = w["L0_conv_bg"]
    v["woT"][0:CI, :] = w["L0_conv_Wo"].T
    v = packs["attn"][1]
    for half in range(2):
        v["qkv"][half * C:half * C + C, :] = w["L1_attn_W_attn"]
    v["proj"][0:C, :] = w["L1_attn_W_proj"]
    v["causal"][:] = np.where(p[None, :] > p[:, None], MASKED, 0.0)
    for i in range(2):
        for j, n in enumerate(("g", "b", "m", "v", "be")):
            c = (5 * i + j) * 4
            v["bn"][:, c:c + 4] = w[f"L1_ffn_{n}{i + 1}"].reshape(4, P).T
    v = packs["ffn"][1]
    for half in range(2):
        v["w1"][half * C:half * C + C, :] = w["L1_ffn_W1"].transpose(1, 0, 2).reshape(C, E * C)
        v["wr"][half * C:half * C + C, :] = w["L1_ffn_Wr"]
    for e in range(E):
        rows, c = (e % 2) * C, e // 2 * P + (e % 2) * C
        v["w2"][rows:rows + C, c:c + C] = w["L1_ffn_W2"][e]
    v["wo"][:] = w["L1_ffn_Wo"].reshape(4, P, C).transpose(1, 0, 2).reshape(P, 4 * C)
    v["br"][0, :] = w["L1_ffn_br"]
    for half in range(2):
        v["bo"][half * E:half * E + E, :] = w["L1_ffn_bo"]
    return {"x1": x1} | {f"pack_{pack}": packs[pack][0] for pack in packs}


def conv_attention_moe(nc, a):
    B, C, H, W = a["out"].shape
    N = H * W
    CI, E = SHAPES["CI"], SHAPES["E"]
    NB = N // P
    HEADS, HS = 4, C // 4
    PAIRS = E * C // P
    assert (B, C, N, CI, NB, E, PAIRS) == (4, 64, 256, 32, 2, 8, 4)
    SB = 2
    VW = P + HS
    CX = 2 * C + 1

    with ExitStack() as ctx:
        def sb(name, shape, dt=F32):
            return ctx.enter_context(nc.sbuf_tensor(name, shape, dt))

        def ps(name, shape):
            return ctx.enter_context(nc.psum_tensor(name, shape, F32))

        def sem(name):
            return ctx.enter_context(nc.semaphore(name))

        packs = {}
        for pack in PACKS:
            at, n = columns(pack)
            tile = sb(f"pack_{pack}", [ROWS.get(pack, P), n])
            packs[pack] = tile
            packs |= {f"{pack}.{name}": tile[:, at[name]] for name in at}
        ident = packs["ident.ident"]
        role = [packs["ident.roles"][:, i:i + 1] for i in range(4)]
        conv_th4 = packs["conv.th4"][0:C + 1, :].rearrange("c (t p) -> c t p", t=2)
        conv_vx = packs["conv.vx"][0:C + 1, :]
        conv_g, conv_woT = packs["conv.g"][0:CI, :], packs["conv.woT"][0:CI, :]
        attn_w, attn_proj = packs["attn.qkv"], packs["attn.proj"][0:C, :]
        bn = packs["attn.bn"].rearrange("p (a v q) -> p a v q", a=2, v=5)
        w1, wr = packs["ffn.w1"], packs["ffn.wr"]
        w2 = packs["ffn.w2"].rearrange("p (q k) -> p q k", q=PAIRS)
        wo = packs["ffn.wo"].rearrange("p (q c) -> p q c", q=PAIRS)
        br, bo = packs["ffn.br"][0:1, :], packs["ffn.bo"][0:2 * E, :]
        neg_ident = sb("neg_ident", [P, P])
        ident_bf = sb("ident_bf", [P, P], BF16)
        causal_bf = sb("causal_bf", [P, P], BF16)
        ones_r = sb("ones_r", [P, P], F32R)
        ones_f = sb("ones_f", [P, P])
        attn_qk = sb("attn_qk", [P, 2, HEADS, HS])
        attn_qk_hi = sb("attn_qk_hi", [P, 2, HEADS, 4, HS], F32R)
        attn_qk_lo = sb("attn_qk_lo", [P, 2, HEADS, 4, HS], F32R)
        attn_v_hi = sb("attn_v_hi", [P, C], F32R)
        attn_v_lo = sb("attn_v_lo", [P, C], F32R)
        w1_hi = sb("w1_hi", [P, E * C], F32R)
        w1_lo = sb("w1_lo", [P, E * C], F32R)
        bn_var = sb("bn_var", [P, 2, PAIRS])
        bn_rs = sb("bn_rs", [P, 2, PAIRS])
        bn_s = sb("bn_s", [P, 2, PAIRS])
        bn_d = sb("bn_d", [P, 2, PAIRS])
        bn_ds = sb("bn_ds", [P, 2, PAIRS])
        bn_c = sb("bn_c", [P, 2, PAIRS])
        wr4 = sb("wr4", [P, E])
        pair_sel = sb("pair_sel", [2 * E, E, C], F32R)
        half = sb("half", [P, 2 * PAIRS])

        warm = sb("warm", [P, 512], BF16)

        def per_batch(name, shape, dt=F32):
            return [sb(f"{name}{b}", shape, dt) for b in range(B)]

        def two(name, shape, dt=F32):
            return [sb(f"{name}{i}", shape, dt) for i in range(2)] * (B // 2)

        x1 = sb("x1", [C + 1, B, N])
        f_tmp = per_batch("f_tmp", [P, 2, N], F32R)
        th_s = per_batch("th_s", [P, N], F32R)
        ph_s = per_batch("ph_s", [P, N], F32R)
        vx = per_batch("vx", [P, NB, CX])
        m1 = per_batch("m1", [P, NB])
        diag1 = per_batch("diag1", [P, NB, P], F32R)
        p1 = per_batch("p1", [P, NB, N])
        r1 = per_batch("r1", [P, NB])
        t1 = per_batch("t1", [P, NB, C])
        t2 = per_batch("t2", [P, NB, C])
        ln = [dict(st=per_batch(f"ln{i}_st", [P, NB, 6]), mv=per_batch(f"ln{i}_mv", [P, NB, 2]),
                   var=per_batch(f"ln{i}_var", [P, NB]), rs=per_batch(f"ln{i}_rs", [P, NB]),
                   xh=per_batch(f"ln{i}_xh", [P, NB, C]), xs=per_batch(f"ln{i}_xs", [P, NB, 2, C]))
              for i in range(2)]
        xT = per_batch("xT", [P, N], F32R)
        x2T = sb("x2T", [P, B, N], F32R)
        qk_tmp = two("qk_tmp", [P, 2, 2 * N], F32R)
        q_s = per_batch("q_s", [P, 2, N], F32R)
        k_s = per_batch("k_s", [P, 2, N], F32R)
        v2 = two("v2", [P, NB, HEADS * VW])
        m2 = per_batch("m2", [P, NB, HEADS])
        diag2 = two("diag2", [P, HEADS, NB, P], F32R)
        p2 = two("p2", [P, 3, 512])
        u_s = two("u_s", [P, N])
        r2 = per_batch("r2", [P, NB, HEADS])
        r2_wide = per_batch("r2_wide", [P, NB, C])
        yT = per_batch("yT", [C, N])
        h1 = sb("h1", [P, PAIRS, B * N])
        xsum = [sb(f"xsum{i}", [P, N]) for i in range(B - 2)]
        gm = sb("gm", [P, NB])
        gl = sb("gl", [P, NB, E])
        ge = sb("ge", [P, NB, E])
        gs = sb("gs", [P, NB])
        gr = sb("gr", [P, NB])
        gws = sb("gws", [P, NB, 2, E])
        gwT = sb("gwT", [2 * E, N], F32R)
        cw = sb("cw", [C, N])
        h2 = sb("h2", [P, PAIRS, B * N])
        o_sb = sb("o_sb", [C, B, N])

        A = ps("A", [P, 3, 512])
        PR = [ps(f"PR{i}", [P, 512]) for i in range(2)]
        Q = [ps(f"Q{i}", [P, 512]) for i in range(2)]
        M = ps("M", [P, 512])
        sums = [A[0:C, 2, :], PR[0][0:C, 0:N], PR[1][0:C, 0:N]]
        pv1 = [Q[(b + 1) % 2][:, 0:NB * (C + 1)].rearrange("p (n c) -> p n c", n=NB) for b in range(B)]
        vps = M[:, 130:130 + NB * C]
        pv2 = M[:, N:2 * N]
        sumsT = M[:, 0:NB * C].rearrange("p (n c) -> p n c", n=NB)
        rT = M[0:C, N:2 * N]

        x_in = [sem(f"x_in{i}") for i in range(2)]
        conv_in, ident_in, attn_in, ffn_in, out_done = map(
            sem, ("conv_in", "ident_in", "attn_in", "ffn_in", "out_done"))
        warm_ok = sem("warm_ok")
        filled = sem("filled")
        v_const = sem("v_const")
        vx_w, vxw_ok = sem("vx_w"), sem("vxw_ok")
        aw_scaled, aw_hi, aw_ok = map(sem, ("aw_scaled", "aw_hi", "aw_ok"))
        w1_rounded, w1_ok = sem("w1_rounded"), sem("w1_ok")
        bn_step, bn_pow, wr_ok, sel_ok = map(sem, ("bn_step", "bn_pow", "wr_ok", "sel_ok"))
        f_ps, vx_ps, f_rnd, f_split, vx_ok = map(sem, ("f_ps", "vx_ps", "f_rnd", "f_split", "vx_ok"))
        s1_ps, m1_ok, d1_ok, s1t_ps, p1_ok, pv1_ps, r1_ok, t1_ok = map(
            sem, ("s1_ps", "m1_ok", "d1_ok", "s1t_ps", "p1_ok", "pv1_ps", "r1_ok", "t1_ok"))
        for i, l in enumerate(ln):
            for n in ("stats", "aggr", "eps", "pow", "xh", "hi", "xs", "T", "TT"):
                l["s_" + n] = sem(f"ln{i}_s_{n}")
        q_ps, k_ps, v_ps, q_rnd, k_rnd, q_ok, k_ok, v_ok = map(
            sem, ("q_ps", "k_ps", "v_ps", "q_rnd", "k_rnd", "q_ok", "k_ok", "v_ok"))
        s2a_ps, s2b_ps, m2_ok, d2a_ok, d2b_ok, s2t_ps, p2_ok = map(
            sem, ("s2a_ps", "s2b_ps", "m2_ok", "d2a_ok", "d2b_ok", "s2t_ps", "p2_ok"))
        pv2_ps, u_ok, sumsT_ps, r2_ok, r2_wide_ok, rT_ps, y_ok, pj_ps, t2_ok = map(
            sem, ("pv2_ps", "u_ok", "sumsT_ps", "r2_ok", "r2_wide_ok", "rT_ps", "y_ok", "pj_ps", "t2_ok"))
        rows_done = sem("rows_done")
        layer_ps, relu_ok, xsum_ok = map(sem, ("layer_ps", "relu_ok", "xsum_ok"))
        g_ps, g_step, g_exp, g_ok, gT_ps, gT_ok, wb_ps, cw_ps, cw_ok = map(
            sem, ("g_ps", "g_step", "g_exp", "g_ok", "gT_ps", "gT_ok", "wb_ps", "cw_ps", "cw_ok"))
        gated, l3_ps, o_ok = map(sem, ("gated", "l3_ps", "o_ok"))

        STEPS, LAG = 13, 2
        FILL = {"loads": 10, 1: 4, 4: 4, "router": 2}

        def schedule(even, odd):
            for slot in range(STEPS + LAG * (B - 1)):
                for step in (even, odd)[slot % 2]:
                    b = (slot - int(step)) // LAG
                    if 0 <= b < B:
                        yield step, b

        def diagonal(engine, out, m):
            n = m.shape[1]
            return engine.tensor_tensor(out, neg_ident[:, :].unsqueeze(1).to_broadcast([P, n, P]),
                                        m.unsqueeze(2).to_broadcast([P, n, P]), ALU.mult)

        def own_columns(v2_b, start):
            return v2_b[:, :, :].rearrange("p n (h c) -> p n h c", h=HEADS)[:, :, :, start:start + HS]

        SETS = [(0, 1), (2,), (3,)]
        OUTPUTS = [(0, 2), (2, 1), (3, 1)]
        SET_ENDS = {batches[-1]: s for s, batches in enumerate(SETS[:-1])}
        LAYERS = 2 * PAIRS

        def layer(s, i, q):
            n = LAYERS * s + PAIRS * i + q
            return n, (Q if s == len(SETS) - 1 else PR)[n % 2][:, 0:len(SETS[s]) * N]

        def columns_of(s):
            return slice(SETS[s][0] * N, (SETS[s][-1] + 1) * N)

        block = ctx.enter_context(nc.Block())

        @block.sync
        def _(sp):
            sp.dma_start(x1[:, 0, :], a["x1"][:, 0, :]).then_inc(x_in[0], 16)
            sp.dma_start(x1[:, 1:B, :], a["x1"][:, 1:B, :]).then_inc(x_in[1], 16)
            sp.dma_start(packs["attn"][:, :], a["pack_attn"]).then_inc(attn_in, 16)
            sp.dma_start(packs["ffn"][:, :], a["pack_ffn"]).then_inc(ffn_in, 16)
            ov = a["out"].rearrange("b c h w -> b c (h w)").rearrange("b c n -> c b n")
            for i, (first, count) in enumerate(OUTPUTS):
                sp.wait_ge(o_ok, i + 1)
                sp.dma_start(ov[:, first:first + count, :], o_sb[:, first:first + count, :]).then_inc(out_done, 16)
            sp.wait_ge(out_done, 16 * len(OUTPUTS))

        @block.gpsimd
        def _(pool):
            pool.memset(ones_f[:, :], 1.0).then_inc(filled, 1)
            pool.memset(half[:, :], -0.5).then_inc(filled, 1)
            for i in range(2):
                pool.memset(v2[i][:, :, :], 0.0).then_inc(filled, 1)
            for i in range(2):
                pool.wait_ge(filled, 3 + i)
                pool.memset(own_columns(v2[i], C), 1.0).then_inc(filled, 1)

            def root(i, b):
                pool.wait_ge(ln[i]["s_eps"], b + 1)
                pool.tensor_tensor(ln[i]["rs"][b][:, :], ln[i]["var"][b][:, :], half[:, 0:NB],
                                   ALU.pow).then_inc(ln[i]["s_pow"], 1)

            for step, b in schedule(even=(10, 6), odd=(9, 7, 3, 1)):
                if step == 1:
                    if b == 0:
                        pool.wait_ge(v_const, 2)
                        pool.wait_ge(filled, 2)
                    pool.wait_ge(m1_ok, b + 1)
                    diagonal(pool, diag1[b][:, :, :], m1[b][:, :]).then_inc(d1_ok, 1)
                if step == 3:
                    root(0, b)
                if step == 7 and b == 0:
                    pool.wait_ge(bn_step, 1)
                    pool.tensor_tensor(bn_rs[:, :, :].rearrange("p a q -> p (a q)"),
                                       bn_var[:, :, :].rearrange("p a q -> p (a q)"), half[:, :],
                                       ALU.pow).then_inc(bn_pow, 1)
                if step == 6:
                    if b > 1:
                        pool.wait_ge(s2t_ps, 2 * (b - 1))
                    pool.wait_ge(m2_ok, NB * b + 1)
                    diagonal(pool, diag2[b][:, :, 0, :], m2[b][:, 0, :]).then_inc(d2a_ok, 1)
                if step == 9:
                    root(1, b)
                if step == 10 and 0 < b < B - 1:
                    pool.wait_ge(ln[1]["s_TT"], b + 1)
                    if b > 1:
                        pool.wait_ge(xsum_ok, b - 1)
                    first = (x2T[:, 0, :].bitcast(F32) if b == 1 else xsum[b - 2][:, :])
                    pool.tensor_tensor(xsum[b - 1][:, :], first, x2T[:, b, :].bitcast(F32),
                                       ALU.add).then_inc(xsum_ok, 1)

        @block.scalar
        def _(act):
            act.dma_start(packs["conv"][:, :], a["pack_conv"]).then_inc(conv_in, 16)
            act.dma_start(packs["ident"][:, :], a["pack_ident"]).then_inc(ident_in, 16)

            def copy(out, in_):
                return act.activation(out, in_, ACT.Copy)

            act.wait_ge(vx_w, 1)
            copy(conv_vx[:, 0:C], Q[1][0:C + 1, 0:C]).then_inc(vxw_ok, 1)

            def relu(s, i, q):
                n, bank = layer(s, i, q)
                out = (h2 if i else h1)[:, q, columns_of(s)]
                act.wait_ge(layer_ps, n + 1)
                act.activation(out, bank, ACT.Relu, bias=bn_c[:, i, q:q + 1],
                               scale=bn_s[:, i, q:q + 1]).then_inc(relu_ok, 1)

            def xT_copy(i, b, out, bank):
                act.wait_ge(ln[i]["s_T"], b + 1)
                copy(out, bank[:, 0:N]).then_inc(ln[i]["s_TT"], 1)

            for step, b in schedule(even=(12, 10, 8, 4, 2, 0, 0.1), odd=(11, 7, 5, 5.1, 5.2)):
                if step == 0:
                    act.wait_ge(f_ps, b + 1)
                    copy(f_tmp[b][:, :, :], Q[b % 2][:, :].rearrange("p (t n) -> p t n", t=2)).then_inc(f_rnd, 1)
                if step == 0.1:
                    act.wait_ge(vx_ps, b + 1)
                    copy(vx[b][:, :, :], PR[0][:, 0:NB * CX].rearrange("p (n c) -> p n c", n=NB)).then_inc(vx_ok, 1)
                if step == 2:
                    act.wait_ge(s1t_ps, b + 1)
                    act.activation(p1[b][:, :, :], Q[b % 2][:, :].rearrange("p (n i) -> p n i", n=NB),
                                   ACT.Exp).then_inc(p1_ok, 1)
                if step == 4:
                    xT_copy(0, b, xT[b][:, :], PR[1])
                if step == 5:
                    act.wait_ge(v_ps, b + 1)
                    act.wait_ge(filled, 5 + b % 2)
                    if b > 1:
                        act.wait_ge(pv2_ps, b - 1)
                    copy(own_columns(v2[b], 0), vps.rearrange("p (n h d) -> p n h d", n=NB, h=HEADS)).then_inc(v_ok, 1)
                if step == 5.1:
                    if b > 1:
                        act.wait_ge(q_ok, b - 1)
                    act.wait_ge(q_ps, b + 1)
                    copy(qk_tmp[b][:, 0, :], PR[0][:, :]).then_inc(q_rnd, 1)
                if step == 5.2:
                    if b > 1:
                        act.wait_ge(k_ok, b - 1)
                    act.wait_ge(k_ps, b + 1)
                    copy(qk_tmp[b][:, 1, :], PR[1][:, :]).then_inc(k_rnd, 1)
                if step == 7:
                    if b > 1:
                        act.wait_ge(pv2_ps, b - 1)
                    for i, banks in enumerate((slice(0, 1), slice(1, 3))):
                        act.wait_ge(s2t_ps, 2 * b + i + 1)
                        act.activation(p2[b][:, banks, :], A[:, banks, :], ACT.Exp).then_inc(p2_ok, 1)
                if step == 8:
                    if b > 1:
                        act.wait_ge(y_ok, b - 1)
                    act.wait_ge(pv2_ps, b + 1)
                    copy(u_s[b][:, :], pv2).then_inc(u_ok, 1)
                if step == 10:
                    xT_copy(1, b, x2T[:, b, :], Q[1])
                if step in (11, 12) and b in SET_ENDS:
                    act.wait_ge(bn_step, 5)
                    for q in range(PAIRS):
                        relu(SET_ENDS[b], step - 11, q)
            last = len(SETS) - 1
            act.wait_ge(g_step, 2)
            act.activation(ge[:, :, :], gl[:, :, :], ACT.Exp).then_inc(g_exp, 1)
            for q in range(PAIRS - 1):
                relu(last, 0, q)
            act.wait_ge(gT_ps, 1)
            copy(gwT[:, :], M[0:2 * E, N:2 * N]).then_inc(gT_ok, 1)
            relu(last, 0, PAIRS - 1)
            relu(last, 1, 0)
            act.wait_ge(cw_ps, 1)
            copy(cw[:, :], M[0:C, 0:N]).then_inc(cw_ok, 1)
            for q in range(1, PAIRS):
                relu(last, 1, q)

        @block.vector
        def _(v):
            def mul_add(out, in0, scalar, in1):
                return v.scalar_tensor_tensor(out=out, in0=in0, scalar=scalar, in1=in1, op0=ALU.mult, op1=ALU.add)

            v.memset(warm[:, :], 0.0).then_inc(warm_ok, 1)
            v.memset(ones_r[:, :].bitcast(F32), 1.0).then_inc(v_const, 1)
            v.wait_ge(ident_in, 16)
            v.tensor_scalar(neg_ident[:, :], ident, -1.0, None, ALU.mult).then_inc(v_const, 1)
            v.tensor_copy(ident_bf[:, :], ident).then_inc(v_const, 1)

            def attention_weights():
                v.wait_ge(attn_in, 16)
                v.tensor_copy(causal_bf[:, :], packs["attn.causal"]).then_inc(v_const, 1)
                v.tensor_scalar(attn_qk[:, 0, :, :], attn_w[:, 0:C].rearrange("p (h d) -> p h d", h=HEADS),
                                float(HS) ** -0.5, None, ALU.mult).then_inc(aw_scaled, 1)
                v.tensor_copy(attn_qk[:, 1, :, :], attn_w[:, C:2 * C].rearrange("p (h d) -> p h d", h=HEADS))\
                    .then_inc(aw_scaled, 1)
                v.tensor_copy(attn_v_hi[:, :], attn_w[:, 2 * C:3 * C]).then_inc(aw_hi, 1)
                v.wait_ge(aw_scaled, 2)
                four = [attn_qk[:, i, :, :].unsqueeze(2).to_broadcast([P, HEADS, 4, HS]) for i in range(2)]
                for i in range(2):
                    v.tensor_copy(attn_qk_hi[:, i, :, :, :], four[i]).then_inc(aw_hi, 1)
                v.wait_ge(aw_hi, 3)
                for i in range(2):
                    v.tensor_tensor(attn_qk_lo[:, i, :, :, :], four[i], attn_qk_hi[:, i, :, :, :].bitcast(F32),
                                    ALU.subtract).then_inc(aw_ok, 1)
                v.tensor_tensor(attn_v_lo[:, :], attn_w[:, 2 * C:3 * C], attn_v_hi[:, :].bitcast(F32),
                                ALU.subtract).then_inc(aw_ok, 1)

            def norm_parameters(part):
                g, bb, m, var, be = (bn[:, :, j, :] for j in range(5))
                if part == 0:
                    v.wait_ge(attn_in, 16)
                    v.tensor_scalar(bn_var[:, :, :], var, EPS_BN, None, ALU.add).then_inc(bn_step, 1)
                    v.tensor_tensor(bn_d[:, :, :], bb, m, ALU.subtract).then_inc(bn_step, 1)
                    return
                v.wait_ge(bn_pow, 1)
                v.tensor_tensor(bn_s[:, :, :], g, bn_rs[:, :, :], ALU.mult).then_inc(bn_step, 1)
                v.wait_ge(bn_step, 3)
                v.tensor_tensor(bn_ds[:, :, :], bn_d[:, :, :], bn_s[:, :, :], ALU.mult).then_inc(bn_step, 1)
                v.wait_ge(bn_step, 4)
                v.tensor_tensor(bn_c[:, :, :], bn_ds[:, :, :], be, ALU.add).then_inc(bn_step, 1)

            def expert_weights():
                v.wait_ge(ffn_in, 16)
                v.tensor_copy(pair_sel[:, :, :], packs["ident.experts"][0:2 * E, :].unsqueeze(2).to_broadcast([2 * E, E, C]))\
                    .then_inc(sel_ok, 1)
                v.tensor_copy(w1_hi[:, :], w1).then_inc(w1_rounded, 1)
                v.tensor_scalar(wr4[:, :], wr, 1.0 / B, None, ALU.mult).then_inc(wr_ok, 1)
                v.wait_ge(w1_rounded, 1)
                v.tensor_tensor(w1_lo[:, :], w1, w1_hi[:, :].bitcast(F32), ALU.subtract).then_inc(w1_ok, 1)

            def layer_norm(i, b, t, ready):
                l = ln[i]
                v.wait_ge(ready, b + 1)
                for n in range(NB):
                    v.bn_stats(l["st"][b][:, n, :], t[:, n, :]).then_inc(l["s_stats"], 1)
                for n in range(NB):
                    v.wait_ge(l["s_stats"], NB * b + n + 1)
                    v.bn_aggr(l["mv"][b][:, n, :], l["st"][b][:, n, :]).then_inc(l["s_aggr"], 1)
                v.wait_ge(l["s_aggr"], NB * (b + 1))
                v.tensor_scalar(l["var"][b][:, :], l["mv"][b][:, :, 1], EPS_LN, None, ALU.add).then_inc(l["s_eps"], 1)

            def normed(i, b, t):
                l = ln[i]
                v.wait_ge(l["s_pow"], b + 1)
                for n in range(NB):
                    v.tensor_scalar(l["xh"][b][:, n, :], t[:, n, :], l["mv"][b][:, n, 0:1], l["rs"][b][:, n:n + 1],
                                    ALU.subtract, ALU.mult).then_inc(l["s_xh"], 1)
                v.wait_ge(l["s_xh"], NB * (b + 1))
                v.tensor_copy(l["xs"][b][:, :, 0, :].bitcast(F32R), l["xh"][b][:, :, :]).then_inc(l["s_hi"], 1)
                v.wait_ge(l["s_hi"], b + 1)
                v.tensor_tensor(l["xs"][b][:, :, 1, :], l["xh"][b][:, :, :], l["xs"][b][:, :, 0, :],
                                ALU.subtract).then_inc(l["s_xs"], 1)

            for step, b in schedule(even=(6, 8.1, 6.1, 8.2, 6.2, 8, 2, 0), odd=(9, 9.1, 7, 5.1, 5.2, 3, 3.1, 1)):
                if step == 0:
                    v.wait_ge(f_rnd, b + 1)
                    for i, (out, r) in enumerate(((th_s, ROLE_THETA), (ph_s, ROLE_PHI))):
                        mul_add(out[b][:, :], f_tmp[b][:, i, :].bitcast(F32), role[r],
                                Q[b % 2][:, i * N:(i + 1) * N]).then_inc(f_split, 1)
                if step == 1:
                    v.wait_ge(s1_ps, b + 1)
                    v.tensor_reduce(m1[b][:, :], Q[(b + 1) % 2][:, :].rearrange("p (n j) -> p n j", n=NB), X,
                                    ALU.max).then_inc(m1_ok, 1)
                if step == 2 and b == 0:
                    attention_weights()
                    norm_parameters(0)
                if step == 3:
                    v.wait_ge(pv1_ps, b + 1)
                    v.reciprocal(r1[b][:, :], pv1[b][:, :, C]).then_inc(r1_ok, 1)
                    v.wait_ge(r1_ok, b + 1)
                    v.wait_ge(vx_ok, b + 1)
                    for n in range(NB):
                        i = mul_add(t1[b][:, n, :], pv1[b][:, n, 0:C], r1[b][:, n:n + 1], vx[b][:, n, C + 1:CX])
                    i.then_inc(t1_ok, 1)
                    layer_norm(0, b, t1[b], t1_ok)
                if step == 3.1:
                    normed(0, b, t1[b])
                if step == 7 and b == 0:
                    expert_weights()
                if step == 8 and b == 0:
                    norm_parameters(1)
                if step in (5.1, 5.2):
                    i = int(step == 5.2)
                    out, r, rnd, ok = ((q_s, ROLE_Q, q_rnd, q_ok), (k_s, ROLE_K, k_rnd, k_ok))[i]
                    v.wait_ge(rnd, b + 1)
                    mul_add(out[b][:, :, :].rearrange("p g n -> p (g n)"), qk_tmp[b][:, i, :].bitcast(F32),
                            role[r], PR[i][:, :]).then_inc(ok, 1)
                if step == 6:
                    v.wait_ge(s2a_ps, b + 1)
                    v.tensor_reduce(m2[b][:, 0, :], A[:, 0, :].rearrange("p (h j) -> p h j", h=HEADS), X,
                                    ALU.max).then_inc(m2_ok, 1)
                if step == 6.1:
                    v.wait_ge(s2b_ps, 2 * (b + 1))
                    v.tensor_reduce(m2[b][:, 1, :].rearrange("p (g t) -> p t g", t=2),
                                    A[:, 1:3, :].rearrange("p t (g j) -> p t g j", g=2), X,
                                    ALU.max).then_inc(m2_ok, 1)
                if step == 6.2:
                    if b > 1:
                        v.wait_ge(s2t_ps, 2 * (b - 1))
                    if b == 0:
                        v.wait_ge(v_const, 2)
                    v.wait_ge(m2_ok, NB * (b + 1))
                    diagonal(v, diag2[b][:, :, 1, :], m2[b][:, 1, :]).then_inc(d2b_ok, 1)
                if step == 8.1:
                    v.wait_ge(sumsT_ps, b + 1)
                    v.reciprocal(r2[b][:, :, :], sumsT.rearrange("p n (h d) -> p n h d", h=HEADS)[:, :, :, 0])\
                        .then_inc(r2_ok, 1)
                    v.wait_ge(r2_ok, b + 1)
                    v.tensor_copy(r2_wide[b][:, :, :].rearrange("p n (h d) -> p n h d", h=HEADS),
                                  r2[b][:, :, :].unsqueeze(3).to_broadcast([P, NB, HEADS, HS])).then_inc(r2_wide_ok, 1)
                if step == 8.2:
                    v.wait_ge(rT_ps, b + 1)
                    v.tensor_tensor(yT[b][:, :], u_s[b][0:C, :], rT, ALU.mult).then_inc(y_ok, 1)
                if step == 9:
                    v.wait_ge(pj_ps, b + 1)
                    v.tensor_tensor(t2[b][:, :, :], Q[0][:, 0:NB * C].rearrange("p (n c) -> p n c", n=NB),
                                    t1[b][:, :, :], ALU.add).then_inc(t2_ok, 1)
                    layer_norm(1, b, t2[b], t2_ok)
                if step == 9.1:
                    normed(1, b, t2[b])
            v.wait_ge(g_ps, 1)
            logits = M[:, 0:NB * E].rearrange("p (n e) -> p n e", n=NB)
            v.tensor_reduce(gm[:, :], logits, X, ALU.max).then_inc(g_step, 1)
            v.wait_ge(g_step, 1)
            v.tensor_tensor(gl[:, :, :], logits, gm[:, :].unsqueeze(2).to_broadcast([P, NB, E]),
                            ALU.subtract).then_inc(g_step, 1)
            v.wait_ge(g_exp, 1)
            v.tensor_reduce(gs[:, :], ge[:, :, :], X, ALU.add).then_inc(g_step, 1)
            v.wait_ge(g_step, 3)
            v.reciprocal(gr[:, :], gs[:, :]).then_inc(g_step, 1)
            v.wait_ge(g_step, 4)
            v.tensor_tensor(gws[:, :, 0, :].bitcast(F32R), ge[:, :, :], gr[:, :].unsqueeze(2).to_broadcast([P, NB, E]),
                            ALU.mult).then_inc(g_step, 1)
            v.wait_ge(g_step, 5)
            for n in range(NB):
                v.scalar_tensor_tensor(out=gws[:, n, 1, :], in0=ge[:, n, :], scalar=gr[:, n:n + 1],
                                       in1=gws[:, n, 0, :], op0=ALU.mult, op1=ALU.subtract).then_inc(g_ok, 1)
            for s in range(B // SB):
                for q in range(PAIRS):
                    v.wait_ge(relu_ok, layer(len(SETS) - 1 if s else 0, 1, q)[0] + 1)
                    v.wait_ge(wb_ps, q // 2 + 1)
                    h = h2[:, q, SB * N * s:SB * N * (s + 1)].rearrange("p (b n) -> p b n", b=SB)
                    v.tensor_tensor(h, h,
                                    A[:, q // 2, (q % 2) * N:(q % 2 + 1) * N].unsqueeze(1).to_broadcast([P, SB, N]),
                                    ALU.mult).then_inc(gated, 1)
            v.wait_ge(cw_ok, 1)
            for i, (first, count) in enumerate(OUTPUTS):
                v.wait_ge(l3_ps, i + 1)
                v.tensor_tensor(o_sb[:, first:first + count, :], sums[i].rearrange("p (b n) -> p b n", b=count),
                                cw[:, :].unsqueeze(1).to_broadcast([C, count, N]), ALU.add).then_inc(o_ok, 1)

        @block.tensor
        def _(pe):
            def mm(out, lhsT, rhs, start=True, stop=True, **k):
                return pe.matmul(out, lhsT, rhs, start=start, stop=stop, **k)

            def keep_busy(step, bank):
                for _ in range(FILL[step]):
                    mm(bank, warm[:, 0:P], warm[:, 0:bank.shape[-1]])

            pe.wait_ge(warm_ok, 1)
            keep_busy("loads", M[:, :])

            pe.wait_ge(conv_in, 16)
            mm(Q[1][0:C + 1, 0:C], conv_g, conv_woT).then_inc(vx_w, 1)

            logits = [M[:, n * E:(n + 1) * E] for n in range(NB)]

            def transposed(i, b, bank):
                pe.wait_ge(ln[i]["s_xs"], b + 1)
                for n in range(NB):
                    last = pe.transpose(bank[:, n * P:(n + 1) * P],
                                        ln[i]["xs"][b][:, n, :, :].rearrange("p t c -> p (t c)"), ident)
                last.then_inc(ln[i]["s_T"], 1)

            def residual(b):
                pe.wait_ge(t2_ok, b + 1)
                for n in range(NB):
                    out, i = (sums[0], b * NB + n) if b < SB else (sums[b - SB + 1], n)
                    mm(out[:, i * P:(i + 1) * P], t2[b][:, n, :], ident, start=(i == 0), stop=False)

            def expert_layer(s, i, q):
                n, bank = layer(s, i, q)
                free = 0 if s == len(SETS) - 1 and i == 0 and q < 2 else n - 1
                ready = layer(s, 0, q)[0] + 1 if i else 0
                if max(free, ready) > 0:
                    pe.wait_ge(relu_ok, max(free, ready))
                if i == 0:
                    for part, w in enumerate((w1_hi, w1_lo)):
                        last = mm(bank, w[:, q * P:(q + 1) * P],
                                  x2T[:, :, :].rearrange("p b n -> p (b n)")[:, columns_of(s)],
                                  start=(part == 0), stop=(part == 1))
                else:
                    last = mm(bank, w2[:, q, :], h1[:, q, columns_of(s)])
                last.then_inc(layer_ps, 1)

            for step, b in schedule(even=(12, 10, 8, 6, 8.1, 4, 8.2, 2, 2.1, 0, 0.1), odd=(11, 9, 7, 7.1, 5, 5.1, 3, 1)):
                if step == 0:
                    pe.wait_ge(x_in[min(b, 1)], 16)
                    if b > 0:
                        pe.wait_ge(m1_ok, b)
                    for i in range(2):
                        last = mm(Q[b % 2][:, i * N:(i + 1) * N], conv_th4[:, i, :], x1[:, b, :])
                    last.then_inc(f_ps, 1)
                if step == 0.1:
                    if b == 0:
                        pe.wait_ge(vxw_ok, 1)
                    else:
                        pe.wait_ge(vx_ok, b)
                    if b >= 3:
                        pe.wait_ge(q_ok, b - 2)
                    for n in range(NB):
                        last = mm(PR[0][:, n * CX:(n + 1) * CX], x1[:, b, n * P:(n + 1) * P], conv_vx)
                    last.then_inc(vx_ps, 1)
                if step == 1:
                    if b > 0:
                        pe.wait_ge(p1_ok, b)
                    if b == 0:
                        pe.wait_ge(vxw_ok, 1)
                    keep_busy(step, Q[(b + 1) % 2][:, :])
                    pe.wait_ge(f_split, 2 * (b + 1))
                    for n in range(NB):
                        last = mm(Q[(b + 1) % 2][:, n * N:(n + 1) * N], th_s[b][:, n * P:(n + 1) * P], ph_s[b][:, :])
                    last.then_inc(s1_ps, 1)
                if step == 2:
                    if b > 0:
                        pe.wait_ge(t1_ok, b)
                    for n in range(NB):
                        mm(Q[b % 2][:, n * N:(n + 1) * N], ph_s[b][:, n * P:(n + 1) * P], th_s[b][:, :],
                           start=(n == 0), stop=False)
                if step == 2.1:
                    pe.wait_ge(d1_ok, b + 1)
                    for n in range(NB):
                        last = mm(Q[b % 2][:, n * N:(n + 1) * N], ones_r[:, :],
                                  diag1[b][:, :, :].rearrange("p n i -> p (n i)"), start=False, stop=(n == NB - 1))
                    last.then_inc(s1t_ps, 1)
                if step == 3:
                    if b < B - 1:
                        pe.wait_ge(f_split, 2 * (b + 2))
                    else:
                        pe.wait_ge(t2_ok, 1)
                    pe.wait_ge(p1_ok, b + 1)
                    pe.wait_ge(vx_ok, b + 1)
                    for i in range(NB):
                        for j in range(NB):
                            last = mm(pv1[b][:, i, :], p1[b][:, j, i * P:(i + 1) * P], vx[b][:, j, 0:C + 1],
                                      start=(j == 0), stop=(j == NB - 1))
                    last.then_inc(pv1_ps, 1)
                if step == 4:
                    if b > 0:
                        pe.wait_ge(k_ok, b)
                    if b == 0:
                        pe.wait_ge(ident_in, 16)
                    keep_busy(step, PR[1][:, :])
                    transposed(0, b, PR[1])
                if step == 5:
                    if b > 1:
                        pe.wait_ge(y_ok, b - 1)
                    if b == 0:
                        pe.wait_ge(aw_ok, 3)
                    pe.wait_ge(ln[0]["s_TT"], b + 1)
                    for n in range(NB):
                        for part, w in enumerate((attn_v_hi, attn_v_lo)):
                            last = mm(vps[:, n * C:(n + 1) * C], xT[b][:, n * P:(n + 1) * P], w[:, :],
                                      start=(part == 0), stop=(part == 1))
                    last.then_inc(v_ps, 1)
                if step == 5.1:
                    pe.wait_ge(ln[0]["s_TT"], b + 1)
                    pe.wait_ge(vx_ok, min(b + 3, B))
                    for i, (bank, ps_sem) in enumerate(((PR[0], q_ps), (PR[1], k_ps))):
                        for g in range(2):
                            for part, w in enumerate((attn_qk_hi, attn_qk_lo)):
                                last = mm(bank[:, g * N:(g + 1) * N],
                                          w[:, i, 2 * g:2 * g + 2, :, :].rearrange("p h r d -> p (h r d)"),
                                          xT[b][:, :], start=(part == 0), stop=(part == 1))
                        last.then_inc(ps_sem, 1)

                def rows(s, h, cols):
                    return s[b][64 * (h % 2):64 * (h % 2) + 64, h // 2, cols]

                def masked_pair(out, t, left, right, cols, mask_l, mask_r, start, stop):
                    for g in range(2):
                        mm(out[:, g, :], rows(left, 2 * g + t, cols), rows(right, 2 * g + t, cols),
                           start=(start and g == 0), stop=False)
                    l, r = mask_l[:, :], mask_r[:, :].unsqueeze(1).to_broadcast([P, 2, P])
                    return mm(out, l, r, start=False, stop=stop)

                first, second, both = slice(0, P), slice(P, N), slice(0, N)
                if step == 6:
                    if b > 0:
                        pe.wait_ge(p2_ok, 2 * b)
                    else:
                        pe.wait_ge(v_const, 4)
                    pe.wait_ge(q_ok, b + 1)
                    pe.wait_ge(k_ok, b + 1)
                    mixed = A[:, 0, :].rearrange("p (g t j) -> p t g j", g=2, t=2)

                    def second_queries(t):
                        bank = A[:, 1 + t, :].rearrange("p (g j) -> p g j", g=2)
                        for g in range(2):
                            mm(bank[:, g, :], rows(q_s, 2 * g + t, second), rows(k_s, 2 * g + t, both),
                               start=(g == 0), stop=False)
                        mm(bank[:, :, second], ident_bf[:, :], causal_bf[:, :].unsqueeze(1).to_broadcast([P, 2, P]),
                           start=False).then_inc(s2b_ps, 1)

                    masked_pair(mixed[:, 0, :, :], 0, q_s, k_s, first, ident_bf, causal_bf, True, False)\
                        .then_inc(rows_done, 1)
                    second_queries(0)
                    pe.wait_ge(rows_done, 2 * b + 1)
                    masked_pair(mixed[:, 1, :, :], 1, q_s, k_s, first, ident_bf, causal_bf, False, True)\
                        .then_inc(s2a_ps, 1)
                    second_queries(1)
                if step == 7:
                    pe.wait_ge(m2_ok, NB * (b + 1))
                    mixed = A[:, 2, :].rearrange("p (g t i) -> p t g i", g=2, t=2)

                    def first_keys(t):
                        bank = A[:, t, :].rearrange("p (g i) -> p g i", g=2)
                        for g in range(2):
                            mm(bank[:, g, :], rows(k_s, 2 * g + t, first), rows(q_s, 2 * g + t, both),
                               start=(g == 0), stop=False)
                        mm(bank[:, :, first], causal_bf[:, :], ident_bf[:, :].unsqueeze(1).to_broadcast([P, 2, P]),
                           start=False, stop=False)

                    masked_pair(mixed[:, 0, :, :], 0, k_s, q_s, second, causal_bf, ident_bf, True, False)\
                        .then_inc(rows_done, 1)
                    first_keys(0)
                    first_keys(1)
                    pe.wait_ge(rows_done, 2 * b + 2)
                    masked_pair(mixed[:, 1, :, :], 1, k_s, q_s, second, causal_bf, ident_bf, False, False)
                if step == 7.1:
                    pe.wait_ge(d2a_ok, b + 1)
                    pe.wait_ge(d2b_ok, b + 1)
                    by_head = diag2[b][:, :, :, :].rearrange("p (g t) n i -> p t g (n i)", t=2)
                    for t in range(2):
                        last = mm(A[:, t, :].rearrange("p (g i) -> p g i", g=2), ones_r[:, :], by_head[:, t, :, :],
                                  start=False)
                        if t == 0:
                            last.then_inc(s2t_ps, 1)
                    mm(A[:, 2, :].rearrange("p (h i) -> p h i", h=HEADS), ones_r[:, :], diag2[b][:, :, 1, :],
                       start=False).then_inc(s2t_ps, 1)
                if step == 8:
                    pe.wait_ge(v_ok, min(b + 2, B))
                    if b > 0:
                        pe.wait_ge(y_ok, b)
                    for k, bank, h in [(0, 0, 0), (0, 0, 2), (0, 1, 1), (0, 1, 3)] + [(1, 2, h) for h in range(HEADS)]:
                        if h < 2:
                            pe.wait_ge(p2_ok, 2 * b + 1 + min(bank, 1))
                        out, weights = (pv2[:, second], p2[b][:, 2, h * P:(h + 1) * P]) if k else \
                            (pv2, p2[b][:, bank, (h // 2) * N:(h // 2 + 1) * N])
                        last = mm(out, v2[b][:, k, h * P:(h + 1) * P], weights, start=(h == 0 and k == 0),
                                  stop=(k == 1 and h == HEADS - 1))
                    last.then_inc(pv2_ps, 1)
                    if b == B - 1:
                        for early in range(SB):
                            residual(early)
                if step == 8.1:
                    pe.wait_ge(u_ok, b + 1)
                    for n in range(NB):
                        last = pe.transpose(sumsT[:, n, :], u_s[b][C:2 * C, n * P:(n + 1) * P], ident[C:2 * C, C:2 * C])
                    last.then_inc(sumsT_ps, 1)
                if step == 8.2:
                    pe.wait_ge(r2_wide_ok, b + 1)
                    for n in range(NB):
                        last = pe.transpose(rT[:, n * P:(n + 1) * P], r2_wide[b][:, n, :], ident)
                    last.then_inc(rT_ps, 1)
                if step == 9:
                    pe.wait_ge(m1_ok, B)
                    if b > 0:
                        pe.wait_ge(t2_ok, b)
                        pe.wait_ge(t1_ok, B)
                    pe.wait_ge(y_ok, b + 1)
                    for n in range(NB):
                        last = mm(Q[0][:, n * C:(n + 1) * C], yT[b][:, n * P:(n + 1) * P], attn_proj)
                    last.then_inc(pj_ps, 1)
                if step == 10:
                    pe.wait_ge(p1_ok, B)
                    if b > 0:
                        pe.wait_ge(ln[1]["s_TT"], b)
                    if b == B - 1:
                        pe.wait_ge(xsum_ok, B - 2)
                        pe.wait_ge(wr_ok, 1)
                        pe.wait_ge(y_ok, B)
                        for n in range(NB):
                            mm(logits[n], xsum[B - 3][:, n * P:(n + 1) * P], wr4[:, :], start=(n == 0), stop=False)
                            mm(logits[n], ones_f[0:1, :], br, start=False, stop=False)
                    transposed(1, b, Q[1])
                if step in (11, 12) and b in SET_ENDS:
                    if step == 11:
                        pe.wait_ge(q_ok, B)
                        pe.wait_ge(k_ok, B)
                        pe.wait_ge(ln[1]["s_TT"], b + 1)
                        pe.wait_ge(w1_ok, 1)
                    for q in range(PAIRS):
                        expert_layer(SET_ENDS[b], step - 11, q)

            def third_layer(i, q):
                first, count = OUTPUTS[i]
                pe.wait_ge(gated, PAIRS * (first // SB) + q + 1)
                last = mm(sums[i], wo[:, q, :], h2[:, q, first * N:(first + count) * N], start=False,
                          stop=(q == PAIRS - 1))
                if q == PAIRS - 1:
                    last.then_inc(l3_ps, 1)

            last_set = len(SETS) - 1
            pe.wait_ge(t2_ok, B)
            keep_busy("router", Q[0][:, :])
            pe.wait_ge(ln[1]["s_TT"], B)
            for n in range(NB):
                last = mm(logits[n], x2T[:, B - 1, n * P:(n + 1) * P].bitcast(F32), wr4[:, :], start=False,
                          stop=(n == NB - 1))
            last.then_inc(g_ps, 1)
            for q in range(PAIRS - 1):
                expert_layer(last_set, 0, q)
            pe.wait_ge(relu_ok, LAYERS * last_set)
            residual(2)
            pe.wait_ge(g_ok, NB)
            for n in range(NB):
                last = pe.transpose(M[0:2 * E, N + n * P:N + (n + 1) * P],
                                    gws[:, n, :, :].rearrange("p t e -> p (t e)"), ident)
            last.then_inc(gT_ps, 1)
            expert_layer(last_set, 0, PAIRS - 1)
            residual(3)
            pe.wait_ge(gT_ok, 1)
            pe.wait_ge(sel_ok, 1)
            for q in range(PAIRS):
                last = mm(A[:, q // 2, (q % 2) * N:(q % 2 + 1) * N],
                          pair_sel[:, 2 * q:2 * q + 2, :].rearrange("e t c -> e (t c)"), gwT[:, :])
                if q % 2:
                    last.then_inc(wb_ps, 1)
            mm(M[0:C, 0:N], bo, gwT[:, :].bitcast(F32)).then_inc(cw_ps, 1)
            for q in range(PAIRS):
                expert_layer(last_set, 1, q)
                third_layer(0, q)
            for i in range(1, len(OUTPUTS)):
                for q in range(PAIRS):
                    third_layer(i, q)


def kernel(**inputs):
    import concourse.bacc as _bacc
    from concourse import mybir as _mybir
    from concourse.bass_utils import run_bass_kernel_spmd as _run

    nc = _bacc.Bacc("TRN2", target_bir_lowering=False, num_devices=1)
    arrays, args = {}, {}
    for name, v in laid_out(inputs).items():
        arrays[f"in_{name}_dram"] = v
        args[name] = nc.dram_tensor(f"in_{name}_dram", v.shape, _mybir.dt.from_np(v.dtype), kind="ExternalInput").ap()
    args["out"] = nc.dram_tensor("out_0_dram", inputs["x"].shape, _mybir.dt.float32, kind="ExternalOutput").ap()
    conv_attention_moe(nc, args)
    r = _run(nc, [arrays], core_ids=[0])
    return r.results[0]["out_0_dram"]
```
